# Optimizing a Trainium2 kernel written in Bass

```python
import numpy as np
import jax
import jax.numpy as jnp

def _softmax(x, axis=-1):
    return jax.nn.softmax(x, axis=axis)

def _gelu(x):
    return jax.nn.gelu(x, approximate=True)

def _silu(x):
    return jax.nn.silu(x)

def _sigmoid(x):
    return jax.nn.sigmoid(x)

def _layernorm(x, axis=-1, eps=1e-05):
    m = jnp.mean(x, axis=axis, keepdims=True)
    v = jnp.var(x, axis=axis, keepdims=True)
    return (x - m) / jnp.sqrt(v + eps)

def _scatter_add(tgt, idx, src, axis=0):
    return tgt.at[idx].add(src)

def _segment_sum(src, seg, n):
    return jax.ops.segment_sum(src, seg, n)
kernel_name = 'mk_adj_resnorm_d1_adj_r2_b74223'

def setup_inputs(seed: int=0):
    np.random.seed(seed)
    _w = jnp.asarray

    def _rec_inputs():
        import jax
        import jax.numpy as jnp
        _gk = jax.random.key(seed)
        x = -0.000125 + 0.9999 * jax.random.normal(jax.random.fold_in(_gk, 1), (16, 512, 512), jnp.float32)
        _a = jax.random.bernoulli(jax.random.fold_in(_gk, 2), 0.0078125, (16, 512, 512))
        _a = jnp.logical_or(_a, jnp.swapaxes(_a, -1, -2))
        _a = jnp.logical_or(_a, jnp.eye(512, dtype=bool))
        _af = _a.astype(jnp.float32)
        _af = _af * jax.random.uniform(jax.random.fold_in(_gk, 3), (16, 512, 512), jnp.float32, 0.05, 0.999994)
        adj = _af
        return (x, adj)
    x, adj = _rec_inputs()

    def _L0_gnn_setup():
        import jax, jax.numpy as jnp
        import numpy as np
        B, N, H, E = (64, 256, 512, 4)
        BN_EPS = 1e-05
        key = jax.random.key(seed)
        ks = jax.random.split(key, 6)
        x = jax.random.normal(ks[0], (B, N, H), dtype=jnp.float32)
        adj = jax.random.uniform(ks[1], (B, N, N), dtype=jnp.float32)
        stdv = 1.0 / np.sqrt(H)
        expert_w = jax.random.uniform(ks[2], (E, H, H), minval=-stdv, maxval=stdv, dtype=jnp.float32)
        r_std = 1.0 / np.sqrt(H)
        router_w = jax.random.uniform(ks[3], (H, E), minval=-r_std, maxval=r_std, dtype=jnp.float32)
        router_b = jax.random.uniform(ks[4], (E,), minval=-r_std, maxval=r_std, dtype=jnp.float32)
        bn_gamma = jnp.ones((E, H), dtype=jnp.float32)
        bn_beta = jnp.zeros((E, H), dtype=jnp.float32)
        return {'x': x, 'adj': adj, 'router_w': router_w, 'router_b': router_b, 'expert_w': expert_w, 'bn_gamma': bn_gamma, 'bn_beta': bn_beta}
    _L0_gnn_all = _L0_gnn_setup()
    _L0_gnn_in = {k: v for k, v in _L0_gnn_all.items() if k in ('router_w', 'router_b', 'expert_w', 'bn_gamma', 'bn_beta')}
    del _L0_gnn_all
    return {'x': x, 'adj': adj, 'L0_gnn_router_w': _L0_gnn_in['router_w'], 'L0_gnn_router_b': _L0_gnn_in['router_b'], 'L0_gnn_expert_w': _L0_gnn_in['expert_w'], 'L0_gnn_bn_gamma': _L0_gnn_in['bn_gamma'], 'L0_gnn_bn_beta': _L0_gnn_in['bn_beta']}

def reference(x, adj, L0_gnn_router_w, L0_gnn_router_b, L0_gnn_expert_w, L0_gnn_bn_gamma, L0_gnn_bn_beta):
    import jax
    import jax.numpy as jnp

    def _L0_gnn_ref(x, adj, router_w, router_b, expert_w, bn_gamma, bn_beta):
        import jax, jax.numpy as jnp
        import numpy as np
        B, N, H, E = (64, 256, 512, 4)
        BN_EPS = 1e-05
        scores = x.mean(axis=1) @ router_w + router_b
        top1 = jnp.argmax(scores, axis=-1)
        n_exp = expert_w.shape[0]
        W = expert_w[top1]
        support = jnp.einsum('bnh,bhk->bnk', x, W)
        out = jnp.einsum('bnm,bmk->bnk', adj, support)
        s = jax.ops.segment_sum(out.sum(axis=1), top1, num_segments=n_exp)
        ss = jax.ops.segment_sum((out * out).sum(axis=1), top1, num_segments=n_exp)
        cnt = jax.ops.segment_sum(jnp.ones_like(top1, dtype=out.dtype), top1, num_segments=n_exp) * out.shape[1]
        cnt = jnp.maximum(cnt, 1.0)[:, None]
        mean = s / cnt
        var = ss / cnt - mean * mean
        m = mean[top1][:, None, :]
        inv = jax.lax.rsqrt(var[top1][:, None, :] + BN_EPS)
        y = (out - m) * inv * bn_gamma[top1][:, None, :] + bn_beta[top1][:, None, :]
        return jax.nn.relu(y)
    x = _layernorm(x + _L0_gnn_ref(x, adj, L0_gnn_router_w, L0_gnn_router_b, L0_gnn_expert_w, L0_gnn_bn_gamma, L0_gnn_bn_beta), axis=-1)
    return x

_drawn_inputs = setup_inputs


def setup_inputs(seed=0):
    import zlib

    import numpy as np

    out = dict(_drawn_inputs(seed))
    spreads = {'L0_gnn_bn_gamma': (1.0, 0.2), 'L0_gnn_bn_beta': (0.0, 0.1)}
    factors = {}
    for name, (base, spread) in spreads.items():
        noise = np.random.default_rng([zlib.crc32(name.encode()), seed]).standard_normal(out[name].shape)
        drawn = base * np.exp(spread * noise) if base else spread * noise
        out[name] = jnp.asarray(drawn.astype(out[name].dtype))
    for name, factor in factors.items():
        out[name] = (out[name] * factor).astype(out[name].dtype)
    return out
```

```python
from contextlib import ExitStack

import concourse.bass as bass
from concourse import mybir

P = 128
F32 = mybir.dt.float32
F32R = mybir.dt.float32r
I32 = mybir.dt.int32
ALU = mybir.AluOpType
ACT = mybir.ActivationFunctionType
AX_X = mybir.AxisListType.X


def build(nc, x, adj_t, w, router_wt, router_b, gamma, beta, out):
    B, N, H = x.shape
    E = w.shape[0]
    C = H // P
    SLOT = C * N
    LOADS = 4
    X0, OUT0, T0 = 0, 6, 6 + B
    SLOTS = T0 + 2
    BN_EPS = LN_EPS = 1e-5
    assert N == H == C * P

    x_by4 = x.rearrange("b (p c) h -> b p (c h)", c=C)
    adj_by4 = adj_t.rearrange("b (p c) n -> b p (c n)", c=C)
    w_v = w.rearrange("e (c p) k -> e p c k", p=P)
    x_rows = x.rearrange("b (c p) h -> b p c h", p=P)
    out_rows = out.rearrange("b (c p) h -> b p c h", p=P)

    with ExitStack() as ctx:
        def sb(name, shape, dt=F32):
            return ctx.enter_context(nc.sbuf_tensor(name, shape, dt))

        def sem(name):
            return ctx.enter_context(nc.semaphore(name))

        arena = sb("arena", [P, SLOTS * SLOT])
        base = nc.lookup_mloc("arena").addr

        def split_part(name, slot):
            return nc.alloc_sbuf_tensor_at(name, [P, C, N], F32R, offset=base + slot * SLOT * 4)

        xhi, xlo = split_part("xhi", 0), split_part("xlo", 1)
        ahi, alo = split_part("ahi", 2), split_part("alo", 3)
        whi, wlo = split_part("whi", 4), split_part("wlo", 5)
        thi, tlo = split_part("thi", T0), split_part("tlo", T0 + 1)

        def slot(s, c=None, n=1):
            if c is None:
                return arena[:, bass.ds(s * SLOT, SLOT)]
            return arena[:, bass.ds(s * SLOT + c * N, n * N)]

        x_stage, a_stage, w_stage = OUT0 + B - 2, OUT0 + B - 1, 5

        rw = sb("router_w_rows", [P, E, H])
        rb = sb("router_b_rows", [P, E])
        gb = sb("gamma_beta", [P, 2, E, C])
        xsum = sb("xsum", [P, H])
        junk = sb("junk", [P, H])
        racc = sb("router_partial", [P, E])
        ones = sb("ones", [P, P])
        ident = sb("ident", [P, P])
        scores = sb("scores", [P, E])
        best = sb("best", [P, 1])
        rank = sb("rank", [P, E])
        high = sb("high", [P, 1])
        down = sb("down", [P, E])
        top1 = sb("top1", [P, B], I32)
        top1f = sb("top1f", [P, B])
        iota = sb("iota", [P, E])
        mask = sb("mask", [P, E, B])
        cnt = sb("cnt", [P, E])
        rcnt = sb("rcnt", [P, E])
        st6 = sb("bn_parts", [P, C, 6])
        half_sq = sb("half_sq", [P, C, 2])
        half_sum = sb("half_sum", [P, C, 2])
        mv = sb("sums_of_batch", [P, B, 2, C])
        tot = sb("expert_sums", [P, E, 2, C])
        avg = sb("expert_means", [P, E, 2, C])
        var = sb("expert_var", [P, E, C])
        std = sb("expert_std", [P, E, C])
        ab = sb("scale_shift", [P, E, 2, C])
        abb = sb("scale_shift_of_batch", [P, 2, C, B])
        eps = sb("eps", [P, 1])
        s1 = [sb(f"rowsum{q}", [P, C]) for q in range(2)]
        nm = [sb(f"negmean{q}", [P, C]) for q in range(2)]
        ssq = [sb(f"rowsq{q}", [P, C]) for q in range(2)]
        sd = [sb(f"rowstd{q}", [P, C]) for q in range(2)]
        rs = [sb(f"rowrstd{q}", [P, C]) for q in range(2)]
        prod = rw[:, 0, :]
        squares = [junk[:, :]] + [rw[:, e, :] for e in range(1, C)]

        bank = [ctx.enter_context(nc.psum_tensor(f"bank{i}", [P, 512], F32)) for i in range(8)]
        t_bank, o_bank = bank[:4], bank[4:]
        scores_ps = t_bank[C - 1]

        loaded_const = sem("loaded_const")
        loaded_x, loaded_a, loaded_w = sem("loaded_x"), sem("loaded_a"), sem("loaded_w")
        const_set = sem("const_set")
        ident_set = sem("ident_set")
        xhi_done, ahi_done, whi_done, thi_done = sem("xhi_done"), sem("ahi_done"), sem("whi_done"), sem("thi_done")
        xlo_done, alo_done, wlo_done, tlo_done = sem("xlo_done"), sem("alo_done"), sem("wlo_done"), sem("tlo_done")
        xsum_step, xsum_done, racc_done = sem("xsum_step"), sem("xsum_done"), sem("racc_done")
        scores_done, scores_read = sem("scores_done"), sem("scores_read")
        best_done, rank_done, high_done, top1_done = sem("best_done"), sem("rank_done"), sem("high_done"), sem("top1_done")
        t_full = sem("t_full")
        t_used = sem("t_used")
        o_full = sem("o_full")
        o_kept = sem("o_kept")
        bn_done, half_step, mv_done = sem("bn_done"), sem("half_step"), sem("mv_done")
        coef_step = sem("coef_step")
        var_done, std_done = sem("var_done"), sem("std_done")
        coef_done = sem("coef_done")
        loaded_row = [sem(f"loaded_row{q}") for q in range(LOADS)]
        aff_v, aff_a = sem("aff_v"), sem("aff_a")
        turned = sem("turned")
        summed = sem("summed")
        nm_done, sq_done, sd_done, rs_done = sem("nm_done"), sem("sq_done"), sem("sd_done"), sem("rs_done")
        fin_done = sem("fin_done")
        stored = sem("stored")

        AFF_DVE = 2
        AFF_ACT = C - AFF_DVE

        block = ctx.enter_context(nc.Block())

        @block.sync
        def _(sp):
            def load_xa(i, first=False):
                if not first:
                    sp.wait_ge(xlo_done, i)
                    sp.wait_ge(xsum_done, i)
                sp.dma_start(slot(x_stage), x_by4[bass.ds(i, 1)].rearrange("b p f -> (b p) f")).then_inc(loaded_x, 16)
                if not first:
                    sp.wait_ge(alo_done, i)
                sp.dma_start(slot(a_stage), adj_by4[bass.ds(i, 1)].rearrange("b p f -> (b p) f")).then_inc(loaded_a, 16)

            load_xa(0, first=True)
            sp.dma_start(rw[:, :, :].rearrange("p e h -> p (e h)"), router_wt.partition_broadcast(P)).then_inc(loaded_const, 16)
            sp.dma_start(rb[:, :], router_b.partition_broadcast(P)).then_inc(loaded_const, 16)
            sp.dma_start(gb[:, 0], gamma).then_inc(loaded_const, 16)
            sp.dma_start(gb[:, 1], beta).then_inc(loaded_const, 16)
            load_xa(1)
            with sp.Fori(2, B) as i:
                load_xa(i)

            def load_rows(j, q):
                sp.dma_start(slot(X0 + j).rearrange("p (c h) -> p c h", c=C),
                             x_rows[bass.ds(j, 1)].rearrange("b p c h -> (b p) c h")).then_inc(loaded_row[q], 16)

            def store_rows(j):
                sp.wait_ge(fin_done, C * (j + 1))
                sp.dma_start(out_rows[bass.ds(j, 1)].rearrange("b p c h -> (b p) c h"),
                             slot(X0 + j).rearrange("p (c h) -> p c h", c=C)).then_inc(stored, 16)

            sp.wait_ge(t_full, C * B)
            for j in range(LOADS):
                load_rows(j, j)
            with sp.Fori(0, B - 2 * LOADS + 1, LOADS) as j0:
                for q in range(LOADS):
                    j = j0 + q
                    sp.wait_ge(summed, C * (j + 1))
                    load_rows(j + LOADS, q)
                    store_rows(j)
            for j in range(B - LOADS, B):
                store_rows(j)
            sp.wait_ge(stored, 16 * B)

        @block.gpsimd
        def _(pool):
            nc.gpsimd.memset(ident[:, :], 0.0).then_inc(ident_set, 1)
            pool.wait_ge(ident_set, 1)
            nc.gpsimd.affine_select(out=ident[:, :], in_=ident[:, :], compare_op=ALU.not_equal, fill=1.0, base=0,
                                    pattern=[[-1, P]], channel_multiplier=1).then_inc(ident_set, 1)

            def load_w(i, first=False):
                pool.wait_ge(top1_done, i + 1)
                if not first:
                    pool.wait_ge(o_full, C * i)
                e = pool.value_load(top1[0:1, bass.ds(i, 1)], min_val=0, max_val=E - 1)
                pool.dma_start(slot(w_stage).rearrange("p (c k) -> p c k", c=C),
                             w_v[bass.ds(e, 1)].rearrange("e p c k -> (e p) c k")).then_inc(loaded_w, 16)

            def sum_x(i, first=False):
                pool.wait_ge(loaded_x, 16 * (i + 1))
                if not first:
                    pool.wait_ge(racc_done, E * i)
                nc.gpsimd.tensor_tensor(xsum[:, :], slot(x_stage, 0), slot(x_stage, 1), ALU.add).then_inc(xsum_step, 1)
                for c in range(2, C):
                    pool.wait_ge(xsum_step, (C - 2) * i + c - 1)
                    nc.gpsimd.tensor_tensor(xsum[:, :], xsum[:, :], slot(x_stage, c),
                                            ALU.add).then_inc(xsum_done if c == C - 1 else xsum_step, 1)

            sum_x(0, first=True)
            sum_x(1)
            load_w(0, first=True)
            with pool.Fori(1, B - 1) as i:
                sum_x(i + 1)
                load_w(i)
            load_w(B - 1)

        @block.scalar
        def _(act):
            def split_hi(dst, stage, loaded, used, used_at, done, i, first=False):
                act.wait_ge(loaded, 16 * (i + 1))
                if not first:
                    act.wait_ge(used, used_at)
                nc.scalar.activation(dst[:, :, :].rearrange("p c n -> p (c n)"), slot(stage), ACT.Copy).then_inc(done, 1)

            def x_hi(i, first=False):
                split_hi(xhi, x_stage, loaded_x, t_full, C * i, xhi_done, i, first)

            def a_hi(i, first=False):
                split_hi(ahi, a_stage, loaded_a, t_full, C * i, ahi_done, i, first)

            def w_hi(i, first=False):
                split_hi(whi, w_stage, loaded_w, o_full, C * i, whi_done, i, first)

            def t_hi(i, c, first=False):
                act.wait_ge(t_full, C * i + c + 1)
                if not first and c < C - 1:
                    act.wait_ge(t_used, (C - 1) * (i - 1) + c + 1)
                elif not first:
                    act.wait_ge(o_full, C * i)
                nc.scalar.activation(thi[:, c, :], t_bank[c][:, :], ACT.Copy).then_inc(thi_done, 1)

            def keep(i):
                for c in range(C):
                    act.wait_ge(o_full, C * i + c + 1)
                    nc.scalar.activation(slot(OUT0 + i, c), o_bank[c][:, :], ACT.Copy).then_inc(o_kept, 1)

            def step(i, keeps=True, w=True, following=True, first=False):
                if keeps:
                    keep(i - 2)
                if w:
                    w_hi(i - 1, first=isinstance(i, int) and i == 1)
                if following:
                    x_hi(i + 1)
                t_hi(i, 0, first)
                if following:
                    a_hi(i + 1)
                for c in range(1, C):
                    t_hi(i, c, first)

            x_hi(0, first=True)
            a_hi(0, first=True)
            step(0, keeps=False, w=False, first=True)
            step(1, keeps=False)
            with act.Fori(2, B - 1) as i:
                step(i)
            step(B - 1, following=False)
            keep(B - 2)
            w_hi(B - 1)
            keep(B - 1)

            act.wait_ge(var_done, 1)
            nc.scalar.activation(std[:, :, :], var[:, :, :], ACT.Sqrt, bias=eps[:, 0:1]).then_inc(std_done, 1)

            def affine(j, q, first=False):
                if not first:
                    act.wait_ge(turned, C * (j - 1))
                for c in range(AFF_DVE, C):
                    nc.scalar.activation(slot(T0 + q, c), slot(OUT0 + j, c), ACT.Identity,
                                         bias=abb[:, 1, c, bass.ds(j, 1)],
                                         scale=abb[:, 0, c, bass.ds(j, 1)]).then_inc(aff_a, 1)

            def rows(j, q):
                act.wait_ge(nm_done, j + 1)
                for c in range(C):
                    nc.scalar.activation(squares[c], slot(X0 + j, c), ACT.Square, bias=nm[q][:, c:c + 1],
                                         accum_out=ssq[q][:, c:c + 1]).then_inc(sq_done, 1)
                act.wait_ge(sq_done, C * (j + 1))
                if not (isinstance(j, int) and j < 2):
                    act.wait_ge(rs_done, j - 1)
                nc.scalar.activation(sd[q][:, :], ssq[q][:, :], ACT.Sqrt, bias=eps[:, 0:1],
                                     scale=1.0 / H).then_inc(sd_done, 1)

            act.wait_ge(coef_done, 1)
            affine(0, 0, first=True)
            affine(1, 1, first=True)
            rows(0, 0)
            affine(2, 0)
            rows(1, 1)
            with act.Fori(2, B - 3, 2) as j0:
                for q in range(2):
                    affine(j0 + q + 1, 1 - q)
                    rows(j0 + q, q)
            affine(B - 1, 1)
            rows(B - 2, 0)
            rows(B - 1, 1)

        @block.vector
        def _(dve):
            nc.vector.memset(ones[:, :], 1.0).then_inc(const_set, 1)
            nc.vector.memset(eps[:, :], BN_EPS).then_inc(const_set, 1)
            for e in range(E):
                nc.vector.memset(iota[:, e:e + 1], float(e)).then_inc(const_set, 1)
                nc.vector.memset(down[:, e:e + 1], float(E - e)).then_inc(const_set, 1)

            def flat(t):
                return t[:, :, :].rearrange("p c n -> p (c n)")

            def x_lo(i):
                dve.wait_ge(xhi_done, i + 1)
                nc.vector.tensor_tensor(flat(xlo), slot(x_stage), flat(xhi).bitcast(F32), ALU.subtract).then_inc(xlo_done, 1)

            def a_lo(i):
                dve.wait_ge(ahi_done, i + 1)
                nc.vector.tensor_tensor(flat(alo), slot(a_stage), flat(ahi).bitcast(F32), ALU.subtract).then_inc(alo_done, 1)

            def w_lo(i):
                dve.wait_ge(whi_done, i + 1)
                nc.vector.tensor_tensor(flat(wlo), slot(w_stage), flat(whi).bitcast(F32), ALU.subtract).then_inc(wlo_done, 1)

            def t_lo(i, c):
                dve.wait_ge(thi_done, C * i + c + 1)
                nc.vector.tensor_tensor(tlo[:, c, :], t_bank[c][:, :], thi[:, c, :].bitcast(F32),
                                        ALU.subtract).then_inc(tlo_done, 1)

            def route(i, first=False):
                if first:
                    dve.wait_ge(loaded_const, 64)
                else:
                    dve.wait_ge(scores_done, i)
                dve.wait_ge(xsum_done, i + 1)
                for e in range(E):
                    if e or not first:
                        dve.wait_ge(racc_done, E * i + e)
                    nc.vector.tensor_tensor_reduce(junk[:, :], xsum[:, :], rw[:, e, :], 1.0, 0.0, ALU.mult, ALU.add,
                                                   racc[:, e:e + 1]).then_inc(racc_done, 1)

            def pick(i, first=False):
                dve.wait_ge(scores_done, i + 1)
                if first:
                    dve.wait_ge(const_set, 2 + 2 * E)
                else:
                    dve.wait_ge(top1_done, i)
                nc.vector.scalar_tensor_tensor(scores[:, :], scores_ps[:, 0:E], 1.0 / N, rb[:, :], ALU.mult,
                                               ALU.add).then_inc(scores_read, 1)
                dve.wait_ge(scores_read, i + 1)
                nc.vector.tensor_reduce(best[:, :], scores[:, :], AX_X, ALU.max).then_inc(best_done, 1)
                dve.wait_ge(best_done, i + 1)
                nc.vector.scalar_tensor_tensor(rank[:, :], scores[:, :], best[:, 0:1], down[:, :], ALU.is_ge,
                                               ALU.mult).then_inc(rank_done, 1)
                dve.wait_ge(rank_done, i + 1)
                nc.vector.tensor_reduce(high[:, :], rank[:, :], AX_X, ALU.max).then_inc(high_done, 1)
                dve.wait_ge(high_done, i + 1)
                nc.vector.tensor_scalar(top1[:, bass.ds(i, 1)], high[:, :], -1.0, float(E), ALU.mult,
                                        ALU.add).then_inc(top1_done, 1)

            def bn(i, first=False):
                for c in range(C):
                    dve.wait_ge(o_kept, C * i + c + 1)
                    if not first and not c:
                        dve.wait_ge(mv_done, 2 * i)
                    nc.vector.bn_stats(st6[:, c, :], slot(OUT0 + i, c)).then_inc(bn_done, 1)
                m, v = (st6[:, :, :].rearrange("p c (h s) -> p c h s", h=2)[:, :, :, t] for t in (1, 2))
                dve.wait_ge(bn_done, C * (i + 1))
                nc.vector.tensor_tensor(half_sq[:, :, :], m, m, ALU.mult).then_inc(half_step, 1)
                nc.vector.tensor_tensor(mv[:, bass.ds(i, 1), 0].rearrange("p b c -> p (b c)"), m[:, :, 0], m[:, :, 1],
                                        ALU.add).then_inc(mv_done, 1)
                dve.wait_ge(half_step, 2 * i + 1)
                nc.vector.scalar_tensor_tensor(half_sum[:, :, :], half_sq[:, :, :], N / 2, v, ALU.mult,
                                               ALU.add).then_inc(half_step, 1)
                dve.wait_ge(half_step, 2 * i + 2)
                nc.vector.tensor_tensor(mv[:, bass.ds(i, 1), 1].rearrange("p b c -> p (b c)"), half_sum[:, :, 0],
                                        half_sum[:, :, 1], ALU.add).then_inc(mv_done, 1)

            def step(i, stats=True, w=True, following=True, first=False):
                if stats:
                    bn(i - 2, first=isinstance(i, int) and i == 2)
                if w:
                    w_lo(i - 1)
                pick(i, first)
                if following:
                    x_lo(i + 1)
                t_lo(i, 0)
                if following:
                    a_lo(i + 1)
                t_lo(i, 1)
                t_lo(i, 2)
                if following:
                    route(i + 1)
                t_lo(i, 3)

            x_lo(0)
            a_lo(0)
            route(0, first=True)
            step(0, stats=False, w=False, first=True)
            step(1, stats=False)
            step(2)
            with dve.Fori(3, B - 1) as i:
                step(i)
            step(B - 1, following=False)
            bn(B - 2)
            w_lo(B - 1)

            count = [0]

            def link(ins):
                count[0] += 1
                ins.then_inc(coef_step, 1)
                dve.wait_ge(coef_step, count[0])

            dve.wait_ge(top1_done, B)
            link(nc.vector.tensor_copy(top1f[:, :], top1[:, :]))
            link(nc.vector.tensor_tensor(mask[:, :, :], iota[:, :].unsqueeze(2).broadcast_to([P, E, B]),
                                         top1f[:, :].unsqueeze(1).broadcast_to([P, E, B]), ALU.is_equal))
            link(nc.vector.tensor_reduce(cnt[:, :], mask[:, :, :], AX_X, ALU.add))
            link(nc.vector.tensor_scalar(cnt[:, :], cnt[:, :], 1.0, None, ALU.max))
            link(nc.vector.reciprocal(rcnt[:, :], cnt[:, :]))
            bn(B - 1)
            dve.wait_ge(mv_done, 2 * B)
            by_expert = prod.rearrange("p (e s b) -> p e s b", e=E, s=2 * C)
            link(nc.vector.tensor_tensor(
                by_expert, mv[:, :, :, :].rearrange("p b s c -> p (s c) b").unsqueeze(1).broadcast_to([P, E, 2 * C, B]),
                mask[:, :, :].unsqueeze(2).broadcast_to([P, E, 2 * C, B]), ALU.mult))
            link(nc.vector.tensor_reduce(tot[:, :, :, :].rearrange("p e s c -> p e (s c)"), by_expert, AX_X, ALU.add))
            for s, scale in enumerate((0.5, 1.0 / N)):
                link(nc.vector.scalar_tensor_tensor(avg[:, :, s], tot[:, :, s], scale,
                                                    rcnt[:, :].unsqueeze(2).broadcast_to([P, E, C]), ALU.mult, ALU.mult))
            mean_e, sq_e = avg[:, :, 0], avg[:, :, 1]
            link(nc.vector.tensor_tensor(var[:, :, :], mean_e, mean_e, ALU.mult))
            nc.vector.tensor_tensor(var[:, :, :], sq_e, var[:, :, :], ALU.subtract).then_inc(var_done, 1)
            dve.wait_ge(std_done, 1)
            link(nc.vector.reciprocal(std[:, :, :], std[:, :, :]))
            link(nc.vector.tensor_tensor(ab[:, :, 0], std[:, :, :], gb[:, 0], ALU.mult))
            link(nc.vector.tensor_tensor(ab[:, :, 1], mean_e, ab[:, :, 0], ALU.mult))
            link(nc.vector.tensor_tensor(ab[:, :, 1], gb[:, 1], ab[:, :, 1], ALU.subtract))
            by_batch = prod.rearrange("p (s b e) -> p s b e", s=2 * C, b=B)
            link(nc.vector.tensor_tensor(
                by_batch,
                ab[:, :, :, :].rearrange("p e s c -> p (s c) e").unsqueeze(2).broadcast_to([P, 2 * C, B, E]),
                mask[:, :, :].rearrange("p e b -> p b e").unsqueeze(1).broadcast_to([P, 2 * C, B, E]), ALU.mult))
            nc.vector.tensor_reduce(abb[:, :, :, :].rearrange("p s c b -> p (s c) b"), by_batch, AX_X,
                                    ALU.add).then_inc(coef_done, 1)
            dve.wait_ge(coef_done, 1)

            def affine(j, q, first=False):
                if not first:
                    dve.wait_ge(turned, C * (j - 1))
                for c in range(AFF_DVE):
                    nc.vector.tensor_scalar(slot(T0 + q, c), slot(OUT0 + j, c), abb[:, 0, c, bass.ds(j, 1)],
                                            abb[:, 1, c, bass.ds(j, 1)], ALU.mult, ALU.add).then_inc(aff_v, 1)

            def rows(j, q, l):
                dve.wait_ge(loaded_row[l], (j - l) * (16 // LOADS) + 16)
                for c in range(C):
                    dve.wait_ge(turned, C * j + c + 1)
                    nc.vector.scalar_tensor_tensor(slot(X0 + j, c), bank[C * q + c][:, :], 0.0, slot(X0 + j, c), ALU.max,
                                                   ALU.add, accum_out=s1[q][:, c:c + 1]).then_inc(summed, 1)
                dve.wait_ge(summed, C * (j + 1))
                if not (isinstance(j, int) and j < 2):
                    dve.wait_ge(fin_done, C * (j - 1))
                nc.vector.tensor_scalar(nm[q][:, :], s1[q][:, :], -1.0 / H, None, ALU.mult).then_inc(nm_done, 1)

            def final(j, q):
                dve.wait_ge(sd_done, j + 1)
                nc.vector.reciprocal(rs[q][:, :], sd[q][:, :]).then_inc(rs_done, 1)
                dve.wait_ge(rs_done, j + 1)
                for c in range(C):
                    nc.vector.tensor_scalar(slot(X0 + j, c), slot(X0 + j, c), nm[q][:, c:c + 1], rs[q][:, c:c + 1],
                                            ALU.add, ALU.mult).then_inc(fin_done, 1)

            affine(0, 0, first=True)
            affine(1, 1, first=True)
            rows(0, 0, 0)
            affine(2, 0)
            rows(1, 1, 1)
            final(0, 0)
            with dve.Fori(2, B - 5, 4) as j0:
                for u in range(4):
                    j, q = j0 + u, u % 2
                    affine(j + 1, 1 - q)
                    rows(j, q, (2 + u) % LOADS)
                    final(j - 1, 1 - q)
            affine(B - 1, 1)
            rows(B - 2, 0, (B - 2) % LOADS)
            final(B - 3, 1)
            rows(B - 1, 1, (B - 1) % LOADS)
            final(B - 2, 0)
            final(B - 1, 1)

        @block.tensor
        def _(pe):
            def product(dst, parts, start, stop):
                (shi, slo), (mhi, mlo) = parts
                nc.tensor.matmul(dst, shi, mhi, start=start, stop=False)
                nc.tensor.matmul(dst, shi, mlo, start=False, stop=False)
                return nc.tensor.matmul(dst, slo, mhi, start=False, stop=stop)

            def aggregate(i, first=False):
                pe.wait_ge(alo_done, i + 1)
                for h in range(C):
                    if not first:
                        pe.wait_ge(tlo_done, C * (i - 1) + h + 1)
                    if h == 1:
                        if not first:
                            pe.wait_ge(tlo_done, C * i)
                        else:
                            pe.wait_ge(const_set, 1)
                        pe.wait_ge(racc_done, E * (i + 1))
                        nc.tensor.matmul(scores_ps[:, 0:E], ones[:, :], racc[:, :], start=True,
                                         stop=True).then_inc(scores_done, 1)
                    if h == C - 1:
                        pe.wait_ge(scores_read, i + 1)
                    for m in range(C):
                        cols = slice(h * P, (h + 1) * P)
                        mm = product(t_bank[h][:, :], ((xhi[:, m, cols], xlo[:, m, cols]), (ahi[:, m, :], alo[:, m, :])),
                                     m == 0, m == C - 1)
                    mm.then_inc(t_full, 1)

            def project(i, first=False):
                pe.wait_ge(wlo_done, i + 1)
                if not first:
                    pe.wait_ge(o_kept, C * i)
                for h in range(C):
                    pe.wait_ge(tlo_done, C * i + h + 1)
                    for k in range(C):
                        cols = slice(k * P, (k + 1) * P)
                        mm = product(o_bank[k][:, :], ((whi[:, h, cols], wlo[:, h, cols]), (thi[:, h, :], tlo[:, h, :])),
                                     h == 0, h == C - 1)
                        if h == C - 1:
                            mm.then_inc(o_full, 1)
                    if h < C - 1:
                        mm.then_inc(t_used, 1)

            aggregate(0, first=True)
            aggregate(1)
            project(0, first=True)
            with pe.Fori(2, B) as i:
                aggregate(i)
                project(i - 1)
            project(B - 1)

            def turn(j, q, first=False):
                pe.wait_ge(aff_v, AFF_DVE * (j + 1))
                pe.wait_ge(aff_a, AFF_ACT * (j + 1))
                for n in range(C):
                    if not first:
                        pe.wait_ge(summed, C * (j - 2) + n + 1)
                    for k in range(C):
                        mm = nc.tensor.transpose(bank[C * q + n][:, k * P:(k + 1) * P],
                                                 arena[:, (T0 + q) * SLOT + k * N + n * P:][:, 0:P], ident[:, :])
                    mm.then_inc(turned, 1)

            pe.wait_ge(ident_set, 2)
            pe.wait_ge(o_kept, C * B)
            turn(0, 0, first=True)
            turn(1, 1, first=True)
            with pe.Fori(2, B - 1, 2) as j0:
                for q in range(2):
                    turn(j0 + q, q)


def kernel(x, adj, L0_gnn_router_w, L0_gnn_router_b, L0_gnn_expert_w, L0_gnn_bn_gamma, L0_gnn_bn_beta):
    import numpy as np
    import concourse.bacc as bacc
    from concourse import mybir as mb
    from concourse.bass_utils import run_bass_kernel_spmd

    E, H = L0_gnn_bn_gamma.shape
    layout = {
        "x": np.ascontiguousarray(x),
        "adj_t": np.ascontiguousarray(np.swapaxes(adj, 1, 2)),
        "w": np.ascontiguousarray(L0_gnn_expert_w),
        "router_wt": np.ascontiguousarray(np.transpose(L0_gnn_router_w)).reshape(-1),
        "router_b": np.ascontiguousarray(L0_gnn_router_b),
        "gamma": np.ascontiguousarray(np.transpose(np.reshape(L0_gnn_bn_gamma, (E, H // 128, 128)), (2, 0, 1))),
        "beta": np.ascontiguousarray(np.transpose(np.reshape(L0_gnn_bn_beta, (E, H // 128, 128)), (2, 0, 1))),
    }
    nc = bacc.Bacc("TRN2", target_bir_lowering=False, num_devices=1)
    aps = [nc.dram_tensor(f"{k}_dram", v.shape, mb.dt.float32, kind="ExternalInput").ap() for k, v in layout.items()]
    out = nc.dram_tensor("out_dram", layout["x"].shape, mb.dt.float32, kind="ExternalOutput").ap()
    build(nc, *aps, out)
    r = run_bass_kernel_spmd(nc, [{f"{k}_dram": v for k, v in layout.items()}], core_ids=[0])
    return r.results[0]["out_dram"]
```

```python
from contextlib import ExitStack

import concourse.bass as bass
from concourse import mybir

P = 128
F32 = mybir.dt.float32
F32R = mybir.dt.float32r
I32 = mybir.dt.int32
ALU = mybir.AluOpType
ACT = mybir.ActivationFunctionType
AX_X = mybir.AxisListType.X


def build(nc, x, adj_t, w, router_wt, router_b, gamma, beta, out):
    B, N, H = x.shape
    E = w.shape[0]
    C = H // P
    SLOT = C * N
    LOADS = 4
    X0, OUT0, T0 = 0, 6, 6 + B
    SLOTS = T0 + 2
    BN_EPS = LN_EPS = 1e-5
    assert N == H == C * P

    x_by4 = x.rearrange("b (p c) h -> b p (c h)", c=C)
    adj_by4 = adj_t.rearrange("b (p c) n -> b p (c n)", c=C)
    w_v = w.rearrange("e (c p) k -> e p c k", p=P)
    x_rows = x.rearrange("b (c p) h -> b p c h", p=P)
    out_rows = out.rearrange("b (c p) h -> b p c h", p=P)

    with ExitStack() as ctx:
        def sb(name, shape, dt=F32):
            return ctx.enter_context(nc.sbuf_tensor(name, shape, dt))

        def sem(name):
            return ctx.enter_context(nc.semaphore(name))

        arena = sb("arena", [P, SLOTS * SLOT])
        base = nc.lookup_mloc("arena").addr

        def split_part(name, slot):
            return nc.alloc_sbuf_tensor_at(name, [P, C, N], F32R, offset=base + slot * SLOT * 4)

        xhi, xlo = split_part("xhi", 0), split_part("xlo", 1)
        ahi, alo = split_part("ahi", 2), split_part("alo", 3)
        whi, wlo = split_part("whi", 4), split_part("wlo", 5)
        thi, tlo = split_part("thi", T0), split_part("tlo", T0 + 1)
        xhi0, xlo0 = split_part("xhi0", OUT0), split_part("xlo0", OUT0 + 1)
        ahi0, alo0 = split_part("ahi0", OUT0 + 2), split_part("alo0", OUT0 + 3)
        whi_last, wlo_last = split_part("whi_last", 2), split_part("wlo_last", 3)

        def slot(s, c=None, n=1):
            if c is None:
                return arena[:, bass.ds(s * SLOT, SLOT)]
            return arena[:, bass.ds(s * SLOT + c * N, n * N)]

        by_chunk = arena[:, :].rearrange("p (s n) -> p s n", n=N)

        x_stage, a_stage, w_stage, w_stage_last = OUT0 + B - 2, OUT0 + B - 1, 5, 3

        rw = sb("router_w_rows", [P, E, H])
        rb = sb("router_b_rows", [P, E])
        gb = sb("gamma_beta", [P, 2, E, C])
        xsum = sb("xsum", [P, H])
        junk = sb("junk", [P, H])
        racc = sb("router_partial", [P, E])
        ones = sb("ones", [P, P])
        ident = sb("ident", [P, P])
        scores = sb("scores", [P, E])
        best = sb("best", [P, 1])
        rank = sb("rank", [P, E])
        high = sb("high", [P, 1])
        down = sb("down", [P, E])
        top1 = sb("top1", [P, B], I32)
        top1f = sb("top1f", [P, B])
        iota = sb("iota", [P, E])
        mask = sb("mask", [P, E, B])
        cnt = sb("cnt", [P, E])
        rcnt = sb("rcnt", [P, E])
        st6 = sb("bn_parts", [P, C, 6])
        half_sq = sb("half_sq", [P, C, 2])
        half_sum = sb("half_sum", [P, C, 2])
        mv = sb("sums_of_batch", [P, B, 2, C])
        tot = sb("expert_sums", [P, E, 2, C])
        avg = sb("expert_means", [P, E, 2, C])
        var = sb("expert_var", [P, E, C])
        std = sb("expert_std", [P, E, C])
        ab = sb("scale_shift", [P, E, 2, C])
        abb = sb("scale_shift_of_batch", [P, 2, C, B])
        eps = sb("eps", [P, 1])
        row_stats = sb("row_stats", [P, 6, 2, C])
        s1, nm, ssq, sd, rs, nmr = ([row_stats[:, t, q] for q in range(2)] for t in range(6))
        weight = xsum[:, 0:2 * E * B].rearrange("p (s e b) -> p s e b", s=2, e=E)
        last_share = xsum[:, 2 * E * B:2 * E * (B + C)].rearrange("p (s e c) -> p s e c", s=2, e=E)
        prod = rw[:, 0, :]
        squares = [junk[:, :]] + [rw[:, e, :] for e in range(1, C)]

        bank = [ctx.enter_context(nc.psum_tensor(f"bank{i}", [P, 512], F32)) for i in range(8)]
        t_bank, o_bank = bank[:4], bank[4:]
        scores_ps = t_bank[C - 1]

        loaded_const = sem("loaded_const")
        loaded_xc = [sem(f"loaded_x_chunk{c}") for c in range(C)]
        loaded_ac = [sem(f"loaded_a_chunk{c}") for c in range(C)]
        loaded_x, loaded_a = sem("loaded_x"), sem("loaded_a")
        loaded_w, loaded_w_last = sem("loaded_w"), sem("loaded_w_last")
        const_set = sem("const_set")
        ident_set = sem("ident_set")
        xhi_done, ahi_done, whi_done, thi_done = sem("xhi_done"), sem("ahi_done"), sem("whi_done"), sem("thi_done")
        xlo_done, alo_done, wlo_done, tlo_done = sem("xlo_done"), sem("alo_done"), sem("wlo_done"), sem("tlo_done")
        xsum_step, xsum_done, racc_done = sem("xsum_step"), sem("xsum_done"), sem("racc_done")
        scores_done, scores_read = sem("scores_done"), sem("scores_read")
        best_done, rank_done, high_done, top1_done = sem("best_done"), sem("rank_done"), sem("high_done"), sem("top1_done")
        t_full = sem("t_full")
        t_used = sem("t_used")
        o_full = sem("o_full")
        o_kept = sem("o_kept")
        bn_done, half_step, mv_done = sem("bn_done"), sem("half_step"), sem("mv_done")
        coef_step = sem("coef_step")
        var_done, std_done = sem("var_done"), sem("std_done")
        coef_done = sem("coef_done")
        loaded_row = [sem(f"loaded_row{q}") for q in range(LOADS)]
        aff_v, aff_a = sem("aff_v"), sem("aff_a")
        turned = sem("turned")
        summed = sem("summed")
        nm_done, sq_done, sd_done, rs_done = sem("nm_done"), sem("sq_done"), sem("sd_done"), sem("rs_done")
        nmr_done = sem("nmr_done")
        fin_done, fin_a = sem("fin_done"), sem("fin_a")
        stored = sem("stored")

        AFF_DVE = 2
        AFF_ACT = C - AFF_DVE
        FIN_DVE = 3
        FIN_ACT = C - FIN_DVE

        block = ctx.enter_context(nc.Block())

        @block.sync
        def _(sp):
            def load_chunks(i):
                for c in range(C):
                    if i:
                        sp.wait_ge(xlo_done, C * (i - 1) + c + 1)
                        sp.wait_ge(xsum_done, i)
                    sp.dma_start(slot(x_stage, c), x_by4[i, :, c * H:(c + 1) * H]).then_inc(loaded_xc[c], 16)
                    if i:
                        sp.wait_ge(alo_done, C * (i - 1) + c + 1)
                    sp.dma_start(slot(a_stage, c), adj_by4[i, :, c * N:(c + 1) * N]).then_inc(loaded_ac[c], 16)

            def load_xa(i):
                sp.wait_ge(xlo_done, C * i)
                sp.wait_ge(xsum_done, i)
                sp.dma_start(slot(x_stage), x_by4[bass.ds(i, 1)].rearrange("b p f -> (b p) f")).then_inc(loaded_x, 16)
                sp.wait_ge(alo_done, C * i)
                sp.dma_start(slot(a_stage), adj_by4[bass.ds(i, 1)].rearrange("b p f -> (b p) f")).then_inc(loaded_a, 16)

            load_chunks(0)
            sp.dma_start(rw[:, :, :].rearrange("p e h -> p (e h)"), router_wt.partition_broadcast(P)).then_inc(loaded_const, 16)
            sp.dma_start(rb[:, :], router_b.partition_broadcast(P)).then_inc(loaded_const, 16)
            sp.dma_start(gb[:, 0], gamma).then_inc(loaded_const, 16)
            sp.dma_start(gb[:, 1], beta).then_inc(loaded_const, 16)
            load_chunks(1)
            with sp.Fori(2, B) as i:
                load_xa(i)

            def load_rows(j, q):
                sp.dma_start(slot(X0 + j).rearrange("p (c h) -> p c h", c=C),
                             x_rows[bass.ds(j, 1)].rearrange("b p c h -> (b p) c h")).then_inc(loaded_row[q], 16)

            def store_rows(j):
                sp.wait_ge(fin_done, FIN_DVE * (j + 1))
                sp.wait_ge(fin_a, FIN_ACT * (j + 1))
                sp.dma_start(out_rows[bass.ds(j, 1)].rearrange("b p c h -> (b p) c h"),
                             slot(X0 + j).rearrange("p (c h) -> p c h", c=C)).then_inc(stored, 16)

            sp.wait_ge(t_full, C * B)
            for j in range(2):
                load_rows(j, j)
            sp.wait_ge(o_full, C * B)
            for j in range(2, LOADS):
                load_rows(j, j)
            with sp.Fori(0, B - 2 * LOADS + 1, LOADS) as j0:
                for q in range(LOADS):
                    j = j0 + q
                    sp.wait_ge(summed, C * (j + 1))
                    load_rows(j + LOADS, q)
                    store_rows(j)
            for j in range(B - LOADS, B - 1):
                store_rows(j)
            for h in range(2):
                sp.wait_ge(fin_done, FIN_DVE * (B - 1) + (C // 2 if h == 0 else FIN_DVE))
                if h:
                    sp.wait_ge(fin_a, FIN_ACT * B)
                cs = slice(h * C // 2, (h + 1) * C // 2)
                sp.dma_start(out_rows[B - 1, :, cs, :],
                             slot(X0 + B - 1).rearrange("p (c h) -> p c h", c=C)[:, cs, :]).then_inc(stored, 16)
            sp.wait_ge(stored, 16 * (B + 1))

        @block.gpsimd
        def _(pool):
            nc.gpsimd.memset(ident[:, :], 0.0).then_inc(ident_set, 1)
            pool.wait_ge(ident_set, 1)
            nc.gpsimd.affine_select(out=ident[:, :], in_=ident[:, :], compare_op=ALU.not_equal, fill=1.0, base=0,
                                    pattern=[[-1, P]], channel_multiplier=1).then_inc(ident_set, 1)

            def load_w(i, first=False, last=False):
                pool.wait_ge(top1_done, i + 1)
                if last:
                    pool.wait_ge(t_full, C * B)
                elif not first:
                    pool.wait_ge(o_full, C * i)
                e = pool.value_load(top1[0:1, bass.ds(i, 1)], min_val=0, max_val=E - 1)
                pool.dma_start(slot(w_stage_last if last else w_stage).rearrange("p (c k) -> p c k", c=C),
                               w_v[bass.ds(e, 1)].rearrange("e p c k -> (e p) c k")).then_inc(loaded_w_last if last else loaded_w, 16)

            def sum_x(i, chunks=False):
                if chunks:
                    pool.wait_ge(loaded_xc[0], 16 * (i + 1))
                    pool.wait_ge(loaded_xc[1], 16 * (i + 1))
                else:
                    pool.wait_ge(loaded_x, 16 * (i - 1))
                if not (chunks and i == 0):
                    pool.wait_ge(racc_done, E * i)
                nc.gpsimd.tensor_tensor(xsum[:, :], slot(x_stage, 0), slot(x_stage, 1), ALU.add).then_inc(xsum_step, 1)
                for c in range(2, C):
                    if chunks:
                        pool.wait_ge(loaded_xc[c], 16 * (i + 1))
                    pool.wait_ge(xsum_step, (C - 2) * i + c - 1)
                    nc.gpsimd.tensor_tensor(xsum[:, :], xsum[:, :], slot(x_stage, c),
                                            ALU.add).then_inc(xsum_done if c == C - 1 else xsum_step, 1)

            sum_x(0, chunks=True)
            sum_x(1, chunks=True)
            load_w(0, first=True)
            with pool.Fori(1, B - 1) as i:
                sum_x(i + 1)
                load_w(i)
            load_w(B - 1, last=True)

        @block.scalar
        def _(act):
            def x_hi(i):
                act.wait_ge(loaded_x, 16 * (i - 1))
                act.wait_ge(t_full, C * i)
                for c in range(C):
                    nc.scalar.activation(xhi[:, c, :], slot(x_stage, c), ACT.Copy).then_inc(xhi_done, 1)

            def a_hi(i):
                act.wait_ge(loaded_a, 16 * (i - 1))
                act.wait_ge(t_full, C * i)
                for c in range(C):
                    nc.scalar.activation(ahi[:, c, :], slot(a_stage, c), ACT.Copy).then_inc(ahi_done, 1)

            def chunk_hi(i, c, x_part, a_part):
                act.wait_ge(loaded_xc[c], 16 * (i + 1))
                nc.scalar.activation(x_part[:, c, :], slot(x_stage, c), ACT.Copy).then_inc(xhi_done, 1)
                act.wait_ge(loaded_ac[c], 16 * (i + 1))
                nc.scalar.activation(a_part[:, c, :], slot(a_stage, c), ACT.Copy).then_inc(ahi_done, 1)

            def w_hi(i, first=False, last=False):
                if last:
                    act.wait_ge(loaded_w_last, 16)
                else:
                    act.wait_ge(loaded_w, 16 * (i + 1))
                if not first and not last:
                    act.wait_ge(o_full, C * i)
                for c in range(C):
                    nc.scalar.activation((whi_last if last else whi)[:, c, :], slot(w_stage_last if last else w_stage, c),
                                         ACT.Copy).then_inc(whi_done, 1)

            def t_hi(i, c, first=False):
                act.wait_ge(t_full, C * i + c + 1)
                if not first and c < C - 1:
                    act.wait_ge(t_used, (C - 1) * (i - 1) + c + 1)
                elif not first:
                    act.wait_ge(o_full, C * i)
                nc.scalar.activation(thi[:, c, :], t_bank[c][:, :], ACT.Copy).then_inc(thi_done, 1)

            def keep(i):
                for c in range(C):
                    act.wait_ge(o_full, C * i + c + 1)
                    nc.scalar.activation(slot(OUT0 + i, c), o_bank[c][:, :], ACT.Copy).then_inc(o_kept, 1)

            def step(i, keeps=True, w=True, following=True, first=False):
                if keeps:
                    keep(i - 2)
                if w:
                    w_hi(i - 1, first=isinstance(i, int) and i == 1)
                if following:
                    x_hi(i + 1)
                t_hi(i, 0, first)
                if following:
                    a_hi(i + 1)
                for c in range(1, C):
                    t_hi(i, c, first)

            for c in range(C):
                chunk_hi(0, c, xhi0, ahi0)
            for c in range(C - 1):
                chunk_hi(1, c, xhi, ahi)
            t_hi(0, 0, first=True)
            t_hi(0, 1, first=True)
            chunk_hi(1, C - 1, xhi, ahi)
            t_hi(0, 2, first=True)
            t_hi(0, 3, first=True)
            step(1, keeps=False)
            with act.Fori(2, B - 1) as i:
                step(i)
            step(B - 1, following=False)
            keep(B - 2)
            w_hi(B - 1, last=True)
            keep(B - 1)

            act.wait_ge(var_done, 1)
            nc.scalar.activation(std[:, :, :], var[:, :, :], ACT.Sqrt, bias=eps[:, 0:1]).then_inc(std_done, 1)

            def affine(j, q, first=False):
                if not first:
                    act.wait_ge(turned, C * (j - 1))
                for c in range(AFF_DVE, C):
                    nc.scalar.activation(slot(T0 + q, c), slot(OUT0 + j, c), ACT.Identity,
                                         bias=abb[:, 1, c, bass.ds(j, 1)],
                                         scale=abb[:, 0, c, bass.ds(j, 1)]).then_inc(aff_a, 1)

            def final(j, q):
                act.wait_ge(nmr_done, j + 1)
                for c in range(FIN_DVE, C):
                    y = by_chunk[:, bass.ds((X0 + j) * C + c, 1), :].rearrange("p a n -> p (a n)")
                    nc.scalar.activation(y, y, ACT.Identity, bias=nmr[q][:, c:c + 1],
                                         scale=rs[q][:, c:c + 1]).then_inc(fin_a, 1)

            def rows(j, q):
                act.wait_ge(nm_done, j + 1)
                for c in range(C):
                    nc.scalar.activation(squares[c], slot(X0 + j, c), ACT.Square, bias=nm[q][:, c:c + 1],
                                         accum_out=ssq[q][:, c:c + 1]).then_inc(sq_done, 1)
                act.wait_ge(sq_done, C * (j + 1))
                if not (isinstance(j, int) and j < 2):
                    act.wait_ge(rs_done, j - 1)
                nc.scalar.activation(sd[q][:, :], ssq[q][:, :], ACT.Sqrt, bias=eps[:, 0:1],
                                     scale=1.0 / H).then_inc(sd_done, 1)

            act.wait_ge(coef_done, 1)
            affine(0, 0, first=True)
            affine(1, 1, first=True)
            rows(0, 0)
            affine(2, 0)
            final(0, 0)
            rows(1, 1)
            with act.Fori(2, B - 3, 2) as j0:
                for q in range(2):
                    affine(j0 + q + 1, 1 - q)
                    final(j0 + q - 1, 1 - q)
                    rows(j0 + q, q)
            affine(B - 1, 1)
            final(B - 3, 1)
            rows(B - 2, 0)
            final(B - 2, 0)
            rows(B - 1, 1)
            final(B - 1, 1)

        @block.vector
        def _(dve):
            nc.vector.memset(ones[:, :], 1.0).then_inc(const_set, 1)
            nc.vector.memset(eps[:, :], BN_EPS).then_inc(const_set, 1)
            for e in range(E):
                nc.vector.memset(iota[:, e:e + 1], float(e)).then_inc(const_set, 1)
                nc.vector.memset(down[:, e:e + 1], float(E - e)).then_inc(const_set, 1)

            def lo(dst, src, hi, c):
                return nc.vector.tensor_tensor(dst[:, c, :], slot(src, c), hi[:, c, :].bitcast(F32), ALU.subtract)

            def x_lo(i):
                for c in range(C):
                    dve.wait_ge(xhi_done, C * i + c + 1)
                    lo(xlo, x_stage, xhi, c).then_inc(xlo_done, 1)

            def a_lo(i):
                for c in range(C):
                    dve.wait_ge(ahi_done, C * i + c + 1)
                    lo(alo, a_stage, ahi, c).then_inc(alo_done, 1)

            def chunk_lo(i, c, x_parts, a_parts):
                dve.wait_ge(xhi_done, C * i + c + 1)
                lo(x_parts[1], x_stage, x_parts[0], c).then_inc(xlo_done, 1)
                dve.wait_ge(ahi_done, C * i + c + 1)
                lo(a_parts[1], a_stage, a_parts[0], c).then_inc(alo_done, 1)

            def w_lo(i, last=False):
                for c in range(C):
                    dve.wait_ge(whi_done, C * i + c + 1)
                    if last:
                        lo(wlo_last, w_stage_last, whi_last, c).then_inc(wlo_done, 1)
                    else:
                        lo(wlo, w_stage, whi, c).then_inc(wlo_done, 1)

            def t_lo(i, c):
                dve.wait_ge(thi_done, C * i + c + 1)
                nc.vector.tensor_tensor(tlo[:, c, :], t_bank[c][:, :], thi[:, c, :].bitcast(F32),
                                        ALU.subtract).then_inc(tlo_done, 1)

            def route(i, first=False):
                if first:
                    dve.wait_ge(loaded_const, 64)
                else:
                    dve.wait_ge(scores_done, i)
                dve.wait_ge(xsum_done, i + 1)
                for e in range(E):
                    if e or not first:
                        dve.wait_ge(racc_done, E * i + e)
                    nc.vector.tensor_tensor_reduce(junk[:, :], xsum[:, :], rw[:, e, :], 1.0, 0.0, ALU.mult, ALU.add,
                                                   racc[:, e:e + 1]).then_inc(racc_done, 1)

            def pick(i, first=False, bank=scores_ps):
                dve.wait_ge(scores_done, i + 1)
                if first:
                    dve.wait_ge(const_set, 2 + 2 * E)
                else:
                    dve.wait_ge(top1_done, i)
                nc.vector.scalar_tensor_tensor(scores[:, :], bank[:, 0:E], 1.0 / N, rb[:, :], ALU.mult,
                                               ALU.add).then_inc(scores_read, 1)
                dve.wait_ge(scores_read, i + 1)
                nc.vector.tensor_reduce(best[:, :], scores[:, :], AX_X, ALU.max).then_inc(best_done, 1)
                dve.wait_ge(best_done, i + 1)
                nc.vector.scalar_tensor_tensor(rank[:, :], scores[:, :], best[:, 0:1], down[:, :], ALU.is_ge,
                                               ALU.mult).then_inc(rank_done, 1)
                dve.wait_ge(rank_done, i + 1)
                nc.vector.tensor_reduce(high[:, :], rank[:, :], AX_X, ALU.max).then_inc(high_done, 1)
                dve.wait_ge(high_done, i + 1)
                nc.vector.tensor_scalar(top1[:, bass.ds(i, 1)], high[:, :], -1.0, float(E), ALU.mult,
                                        ALU.add).then_inc(top1_done, 1)

            def bn(i, first=False):
                for c in range(C):
                    dve.wait_ge(o_kept, C * i + c + 1)
                    if not first and not c:
                        dve.wait_ge(mv_done, 2 * i)
                    nc.vector.bn_stats(st6[:, c, :], slot(OUT0 + i, c)).then_inc(bn_done, 1)
                m, v = (st6[:, :, :].rearrange("p c (h s) -> p c h s", h=2)[:, :, :, t] for t in (1, 2))
                dve.wait_ge(bn_done, C * (i + 1))
                nc.vector.tensor_tensor(half_sq[:, :, :], m, m, ALU.mult).then_inc(half_step, 1)
                nc.vector.tensor_tensor(mv[:, bass.ds(i, 1), 0].rearrange("p b c -> p (b c)"), m[:, :, 0], m[:, :, 1],
                                        ALU.add).then_inc(mv_done, 1)
                dve.wait_ge(half_step, 2 * i + 1)
                nc.vector.scalar_tensor_tensor(half_sum[:, :, :], half_sq[:, :, :], N / 2, v, ALU.mult,
                                               ALU.add).then_inc(half_step, 1)
                dve.wait_ge(half_step, 2 * i + 2)
                nc.vector.tensor_tensor(mv[:, bass.ds(i, 1), 1].rearrange("p b c -> p (b c)"), half_sum[:, :, 0],
                                        half_sum[:, :, 1], ALU.add).then_inc(mv_done, 1)

            def step(i, stats=True, picks=True, following=True):
                if stats:
                    bn(i - 2, first=isinstance(i, int) and i == 2)
                if picks:
                    pick(i)
                w_lo(i - 1)
                if following:
                    x_lo(i + 1)
                t_lo(i, 0)
                if following:
                    a_lo(i + 1)
                t_lo(i, 1)
                t_lo(i, 2)
                if following:
                    route(i + 1)
                t_lo(i, 3)

            for c in range(C):
                chunk_lo(0, c, (xhi0, xlo0), (ahi0, alo0))
            route(0, first=True)
            for c in range(C - 1):
                chunk_lo(1, c, (xhi, xlo), (ahi, alo))
            t_lo(0, 0)
            t_lo(0, 1)
            chunk_lo(1, C - 1, (xhi, xlo), (ahi, alo))
            t_lo(0, 2)
            t_lo(0, 3)
            pick(0, first=True, bank=o_bank[0])
            route(1)
            pick(1, bank=o_bank[1])
            step(1, stats=False, picks=False)
            step(2)
            with dve.Fori(3, B - 1) as i:
                step(i)
            step(B - 1, following=False)
            bn(B - 2)
            w_lo(B - 1, last=True)

            count = [0]

            def link(ins):
                count[0] += 1
                ins.then_inc(coef_step, 1)
                dve.wait_ge(coef_step, count[0])

            dve.wait_ge(top1_done, B)
            dve.wait_ge(mv_done, 2 * (B - 1))
            link(nc.vector.tensor_copy(top1f[:, :], top1[:, :]))
            link(nc.vector.tensor_tensor(mask[:, :, :], iota[:, :].unsqueeze(2).broadcast_to([P, E, B]),
                                         top1f[:, :].unsqueeze(1).broadcast_to([P, E, B]), ALU.is_equal))
            link(nc.vector.tensor_reduce(cnt[:, :], mask[:, :, :], AX_X, ALU.add))
            link(nc.vector.tensor_scalar(cnt[:, :], cnt[:, :], 1.0, None, ALU.max))
            link(nc.vector.reciprocal(rcnt[:, :], cnt[:, :]))
            for s, scale in enumerate((0.5, 1.0 / N)):
                link(nc.vector.scalar_tensor_tensor(weight[:, s], mask[:, :, :], scale,
                                                    rcnt[:, :].unsqueeze(2).broadcast_to([P, E, B]), ALU.mult, ALU.mult))
            for s in range(2):
                by_expert = prod[:, 0:E * C * (B - 1)].rearrange("p (e c b) -> p e c b", e=E, c=C)
                link(nc.vector.tensor_tensor(
                    by_expert, mv[:, 0:B - 1, s].rearrange("p b c -> p c b").unsqueeze(1).broadcast_to([P, E, C, B - 1]),
                    weight[:, s, :, 0:B - 1].unsqueeze(2).broadcast_to([P, E, C, B - 1]), ALU.mult))
                link(nc.vector.tensor_reduce(tot[:, :, s], by_expert, AX_X, ALU.add))
            bn(B - 1)
            dve.wait_ge(mv_done, 2 * B)
            for s in range(2):
                link(nc.vector.tensor_tensor(last_share[:, s], mv[:, B - 1, s].unsqueeze(1).broadcast_to([P, E, C]),
                                             weight[:, s, :, B - 1].unsqueeze(2).broadcast_to([P, E, C]), ALU.mult))
                link(nc.vector.tensor_tensor(avg[:, :, s], tot[:, :, s], last_share[:, s], ALU.add))
            mean_e, sq_e = avg[:, :, 0], avg[:, :, 1]
            link(nc.vector.tensor_tensor(var[:, :, :], mean_e, mean_e, ALU.mult))
            nc.vector.tensor_tensor(var[:, :, :], sq_e, var[:, :, :], ALU.subtract).then_inc(var_done, 1)
            dve.wait_ge(std_done, 1)
            link(nc.vector.reciprocal(std[:, :, :], std[:, :, :]))
            link(nc.vector.tensor_tensor(ab[:, :, 0], std[:, :, :], gb[:, 0], ALU.mult))
            link(nc.vector.tensor_tensor(ab[:, :, 1], mean_e, ab[:, :, 0], ALU.mult))
            link(nc.vector.tensor_tensor(ab[:, :, 1], gb[:, 1], ab[:, :, 1], ALU.subtract))
            by_batch = prod.rearrange("p (s b e) -> p s b e", s=2 * C, b=B)
            link(nc.vector.tensor_tensor(
                by_batch,
                ab[:, :, :, :].rearrange("p e s c -> p (s c) e").unsqueeze(2).broadcast_to([P, 2 * C, B, E]),
                mask[:, :, :].rearrange("p e b -> p b e").unsqueeze(1).broadcast_to([P, 2 * C, B, E]), ALU.mult))
            nc.vector.tensor_reduce(abb[:, :, :, :].rearrange("p s c b -> p (s c) b"), by_batch, AX_X,
                                    ALU.add).then_inc(coef_done, 1)
            dve.wait_ge(coef_done, 1)

            def affine(j, q, first=False):
                if not first:
                    dve.wait_ge(turned, C * (j - 1))
                for c in range(AFF_DVE):
                    nc.vector.tensor_scalar(slot(T0 + q, c), slot(OUT0 + j, c), abb[:, 0, c, bass.ds(j, 1)],
                                            abb[:, 1, c, bass.ds(j, 1)], ALU.mult, ALU.add).then_inc(aff_v, 1)

            def rows(j, q, l):
                dve.wait_ge(loaded_row[l], (j - l) * (16 // LOADS) + 16)
                for c in range(C):
                    dve.wait_ge(turned, C * j + c + 1)
                    nc.vector.scalar_tensor_tensor(slot(X0 + j, c), bank[C * q + c][:, :], 0.0, slot(X0 + j, c), ALU.max,
                                                   ALU.add, accum_out=s1[q][:, c:c + 1]).then_inc(summed, 1)
                dve.wait_ge(summed, C * (j + 1))
                if not (isinstance(j, int) and j < 2):
                    dve.wait_ge(fin_done, FIN_DVE * (j - 1))
                    dve.wait_ge(fin_a, FIN_ACT * (j - 1))
                nc.vector.tensor_scalar(nm[q][:, :], s1[q][:, :], -1.0 / H, None, ALU.mult).then_inc(nm_done, 1)

            def final(j, q):
                dve.wait_ge(sd_done, j + 1)
                nc.vector.reciprocal(rs[q][:, :], sd[q][:, :]).then_inc(rs_done, 1)
                dve.wait_ge(rs_done, j + 1)
                nc.vector.tensor_tensor(nmr[q][:, :], nm[q][:, :], rs[q][:, :], ALU.mult).then_inc(nmr_done, 1)
                for c in range(FIN_DVE):
                    nc.vector.tensor_scalar(slot(X0 + j, c), slot(X0 + j, c), nm[q][:, c:c + 1], rs[q][:, c:c + 1],
                                            ALU.add, ALU.mult).then_inc(fin_done, 1)

            affine(0, 0, first=True)
            affine(1, 1, first=True)
            rows(0, 0, 0)
            affine(2, 0)
            rows(1, 1, 1)
            final(0, 0)
            with dve.Fori(2, B - 5, 4) as j0:
                for u in range(4):
                    j, q = j0 + u, u % 2
                    affine(j + 1, 1 - q)
                    rows(j, q, (2 + u) % LOADS)
                    final(j - 1, 1 - q)
            affine(B - 1, 1)
            rows(B - 2, 0, (B - 2) % LOADS)
            final(B - 3, 1)
            rows(B - 1, 1, (B - 1) % LOADS)
            final(B - 2, 0)
            final(B - 1, 1)

        @block.tensor
        def _(pe):
            def product(dst, parts, start, stop):
                (shi, slo), (mhi, mlo) = parts
                nc.tensor.matmul(dst, shi, mhi, start=start, stop=False)
                nc.tensor.matmul(dst, shi, mlo, start=False, stop=False)
                return nc.tensor.matmul(dst, slo, mhi, start=False, stop=stop)

            def score(i, dst):
                pe.wait_ge(racc_done, E * (i + 1))
                nc.tensor.matmul(dst[:, 0:E], ones[:, :], racc[:, :], start=True, stop=True).then_inc(scores_done, 1)

            def aggregate_0():
                for m in range(C):
                    pe.wait_ge(alo_done, m + 1)
                    for h in range(C):
                        cols = slice(h * P, (h + 1) * P)
                        mm = product(t_bank[h][:, :], ((xhi0[:, m, cols], xlo0[:, m, cols]), (ahi0[:, m, :], alo0[:, m, :])),
                                     m == 0, m == C - 1)
                        if m == C - 1:
                            mm.then_inc(t_full, 1)

            def aggregate(i, scores=True):
                pe.wait_ge(alo_done, C * (i + 1))
                for h in range(C):
                    pe.wait_ge(tlo_done, C * (i - 1) + h + 1)
                    if scores and h == 1:
                        pe.wait_ge(tlo_done, C * i)
                        score(i, scores_ps)
                    if scores and h == C - 1:
                        pe.wait_ge(scores_read, i + 1)
                    for m in range(C):
                        cols = slice(h * P, (h + 1) * P)
                        mm = product(t_bank[h][:, :], ((xhi[:, m, cols], xlo[:, m, cols]), (ahi[:, m, :], alo[:, m, :])),
                                     m == 0, m == C - 1)
                    mm.then_inc(t_full, 1)

            def project(i, first=False):
                if first:
                    pe.wait_ge(scores_read, 2)
                else:
                    pe.wait_ge(o_kept, C * i)
                for h in range(C):
                    pe.wait_ge(wlo_done, C * i + h + 1)
                    pe.wait_ge(tlo_done, C * i + h + 1)
                    for k in range(C):
                        cols = slice(k * P, (k + 1) * P)
                        mm = product(o_bank[k][:, :], ((whi[:, h, cols], wlo[:, h, cols]), (thi[:, h, :], tlo[:, h, :])),
                                     h == 0, h == C - 1)
                        if h == C - 1:
                            mm.then_inc(o_full, 1)
                    if h < C - 1:
                        mm.then_inc(t_used, 1)

            aggregate_0()
            pe.wait_ge(const_set, 1)
            score(0, o_bank[0])
            aggregate(1, scores=False)
            score(1, o_bank[1])
            project(0, first=True)
            with pe.Fori(2, B) as i:
                aggregate(i)
                project(i - 1)
            pe.wait_ge(wlo_done, C * B)
            pe.wait_ge(tlo_done, C * B)
            for k in range(C):
                pe.wait_ge(o_kept, C * (B - 2) + k + 1)
                for h in range(C):
                    cols = slice(k * P, (k + 1) * P)
                    mm = product(o_bank[k][:, :], ((whi_last[:, h, cols], wlo_last[:, h, cols]), (thi[:, h, :], tlo[:, h, :])),
                                 h == 0, h == C - 1)
                mm.then_inc(o_full, 1)

            def turn(j, q, first=False):
                pe.wait_ge(aff_v, AFF_DVE * (j + 1))
                pe.wait_ge(aff_a, AFF_ACT * (j + 1))
                for n in range(C):
                    if not first:
                        pe.wait_ge(summed, C * (j - 2) + n + 1)
                    for k in range(C):
                        mm = nc.tensor.transpose(bank[C * q + n][:, k * P:(k + 1) * P],
                                                 arena[:, (T0 + q) * SLOT + k * N + n * P:][:, 0:P], ident[:, :])
                    mm.then_inc(turned, 1)

            pe.wait_ge(ident_set, 2)
            pe.wait_ge(o_kept, C * B)
            turn(0, 0, first=True)
            turn(1, 1, first=True)
            with pe.Fori(2, B - 1, 2) as j0:
                for q in range(2):
                    turn(j0 + q, q)


def kernel(x, adj, L0_gnn_router_w, L0_gnn_router_b, L0_gnn_expert_w, L0_gnn_bn_gamma, L0_gnn_bn_beta):
    import numpy as np
    import concourse.bacc as bacc
    from concourse import mybir as mb
    from concourse.bass_utils import run_bass_kernel_spmd

    E, H = L0_gnn_bn_gamma.shape
    layout = {
        "x": np.ascontiguousarray(x),
        "adj_t": np.ascontiguousarray(np.swapaxes(adj, 1, 2)),
        "w": np.ascontiguousarray(L0_gnn_expert_w),
        "router_wt": np.ascontiguousarray(np.transpose(L0_gnn_router_w)).reshape(-1),
        "router_b": np.ascontiguousarray(L0_gnn_router_b),
        "gamma": np.ascontiguousarray(np.transpose(np.reshape(L0_gnn_bn_gamma, (E, H // 128, 128)), (2, 0, 1))),
        "beta": np.ascontiguousarray(np.transpose(np.reshape(L0_gnn_bn_beta, (E, H // 128, 128)), (2, 0, 1))),
    }
    nc = bacc.Bacc("TRN2", target_bir_lowering=False, num_devices=1)
    aps = [nc.dram_tensor(f"{k}_dram", v.shape, mb.dt.float32, kind="ExternalInput").ap() for k, v in layout.items()]
    out = nc.dram_tensor("out_dram", layout["x"].shape, mb.dt.float32, kind="ExternalOutput").ap()
    build(nc, *aps, out)
    r = run_bass_kernel_spmd(nc, [{f"{k}_dram": v for k, v in layout.items()}], core_ids=[0])
    return r.results[0]["out_dram"]
```

```python
from contextlib import ExitStack

import concourse.bass as bass
from concourse import mybir

P = 128
F32 = mybir.dt.float32
F32R = mybir.dt.float32r
I32 = mybir.dt.int32
ALU = mybir.AluOpType
ACT = mybir.ActivationFunctionType
AX_X = mybir.AxisListType.X


def build(nc, x, adj_t, w, router_wt, router_b, gamma, beta, out):
    B, N, H = x.shape
    E = w.shape[0]
    C = H // P
    SLOT = C * N
    AHEAD = 6
    RING = AHEAD + 2
    X0, OUT0, T0 = 0, 6, 6 + B
    SLOTS = T0 + 2
    BN_EPS = LN_EPS = 1e-5
    assert N == H == C * P

    x_by4 = x.rearrange("b (p c) h -> b p (c h)", c=C)
    adj_by4 = adj_t.rearrange("b (p c) n -> b p (c n)", c=C)
    w_v = w.rearrange("e (c p) k -> e p c k", p=P)
    x_rows = x.rearrange("b (c p) h -> b p c h", p=P)
    out_rows = out.rearrange("b (c p) h -> b p c h", p=P)

    with ExitStack() as ctx:
        def sb(name, shape, dt=F32):
            return ctx.enter_context(nc.sbuf_tensor(name, shape, dt))

        def sem(name):
            return ctx.enter_context(nc.semaphore(name))

        arena = sb("arena", [P, SLOTS * SLOT])
        base = nc.lookup_mloc("arena").addr

        def split_part(name, slot):
            return nc.alloc_sbuf_tensor_at(name, [P, C, N], F32R, offset=base + slot * SLOT * 4)

        xhi, xlo = split_part("xhi", 0), split_part("xlo", 1)
        ahi, alo = split_part("ahi", 2), split_part("alo", 3)
        whi, wlo = split_part("whi", 4), split_part("wlo", 5)
        thi, tlo = split_part("thi", T0), split_part("tlo", T0 + 1)
        xhi0, xlo0 = split_part("xhi0", OUT0), split_part("xlo0", OUT0 + 1)
        ahi0, alo0 = split_part("ahi0", OUT0 + 2), split_part("alo0", OUT0 + 3)
        whi_last, wlo_last = split_part("whi_last", 2), split_part("wlo_last", 3)

        def slot(s, c=None, n=1):
            if c is None:
                return arena[:, bass.ds(s * SLOT, SLOT)]
            return arena[:, bass.ds(s * SLOT + c * N, n * N)]

        by_chunk = arena[:, :].rearrange("p (s n) -> p s n", n=N)

        x_stage, a_stage, w_stage, w_stage_last = OUT0 + B - 2, OUT0 + B - 1, 5, 3

        rw = sb("router_w_rows", [P, E, H])
        rb = sb("router_b_rows", [P, E])
        gb = sb("gamma_beta", [P, 2, E, C])
        xsum = sb("xsum", [P, H])
        junk = sb("junk", [P, H])
        racc = sb("router_partial", [P, E])
        ones = sb("ones", [P, P])
        ident = sb("ident", [P, P])
        scores = sb("scores", [P, E])
        best = sb("best", [P, 1])
        rank = sb("rank", [P, E])
        high = sb("high", [P, 1])
        down = sb("down", [P, E])
        top1 = sb("top1", [P, B], I32)
        top1f = sb("top1f", [P, B])
        iota = sb("iota", [P, E])
        mask = sb("mask", [P, E, B])
        cnt = sb("cnt", [P, E])
        rcnt = sb("rcnt", [P, E])
        st6 = sb("bn_parts", [P, C, 6])
        half_sq = sb("half_sq", [P, C, 2])
        half_sum = sb("half_sum", [P, C, 2])
        mv = sb("sums_of_batch", [P, B, 2, C])
        tot = sb("expert_sums", [P, E, 2, C])
        avg = sb("expert_means", [P, E, 2, C])
        var = sb("expert_var", [P, E, C])
        std = sb("expert_std", [P, E, C])
        ab = sb("scale_shift", [P, E, 2, C])
        abb = sb("scale_shift_of_batch", [P, 2, C, B])
        eps = sb("eps", [P, 1])
        minus_share = sb("minus_share", [P, C])
        row_stats = sb("row_stats", [P, 6, 2, C])
        s1, nm, ssq, sd, rs, nmr = ([row_stats[:, t, q] for q in range(2)] for t in range(6))
        weight = xsum[:, 0:2 * E * B].rearrange("p (s e b) -> p s e b", s=2, e=E)
        last_share = xsum[:, 2 * E * B:2 * E * (B + C)].rearrange("p (e s c) -> p e s c", s=2, e=E)
        prod = rw[:, 0, :]
        squares = [junk[:, :]] + [rw[:, e, :] for e in range(1, C)]

        bank = [ctx.enter_context(nc.psum_tensor(f"bank{i}", [P, 512], F32)) for i in range(8)]
        t_bank, o_bank = bank[:4], bank[4:]
        scores_ps = t_bank[C - 1]

        loaded_const = sem("loaded_const")
        loaded_xc = [sem(f"loaded_x_chunk{c}") for c in range(C)]
        loaded_ac = [sem(f"loaded_a_chunk{c}") for c in range(C)]
        alo1_done = sem("alo1_done")
        loaded_x, loaded_a = sem("loaded_x"), sem("loaded_a")
        loaded_w, loaded_w_last = sem("loaded_w"), sem("loaded_w_last")
        const_set = sem("const_set")
        ident_set = sem("ident_set")
        share_set = sem("share_set")
        xhi_done, ahi_done, whi_done, thi_done = sem("xhi_done"), sem("ahi_done"), sem("whi_done"), sem("thi_done")
        xlo_done, alo_done, wlo_done, tlo_done = sem("xlo_done"), sem("alo_done"), sem("wlo_done"), sem("tlo_done")
        xsum_step, xsum_done, racc_done = sem("xsum_step"), sem("xsum_done"), sem("racc_done")
        scores_done, scores_read = sem("scores_done"), sem("scores_read")
        best_done, rank_done, high_done, top1_done = sem("best_done"), sem("rank_done"), sem("high_done"), sem("top1_done")
        t_full = sem("t_full")
        t_used = sem("t_used")
        o_full = sem("o_full")
        o_kept = sem("o_kept")
        bn_done, half_step, mv_done = sem("bn_done"), sem("half_step"), sem("mv_done")
        coef_step, spread_step = sem("coef_step"), sem("spread_step")
        var_done, std_done = sem("var_done"), sem("std_done")
        coef_done = sem("coef_done")
        loaded_row = [sem(f"loaded_row{q}") for q in range(RING)]
        aff_v, aff_a = sem("aff_v"), sem("aff_a")
        turned = sem("turned")
        summed = sem("summed")
        nm_done, sq_done, sd_done, rs_done = sem("nm_done"), sem("sq_done"), sem("sd_done"), sem("rs_done")
        nmr_done = sem("nmr_done")
        fin_done, fin_a = sem("fin_done"), sem("fin_a")
        stored = sem("stored")

        AFF_DVE = (2, 3)
        AFF_ACT = tuple(C - a for a in AFF_DVE)
        RECIP_AT = 3
        FIRST = 2
        FIN_DVE = 3
        FIN_ACT = C - FIN_DVE
        BY_CHUNK = 3

        def through(shares, pairs, q):
            return sum(shares) * pairs + sum(shares[:q + 1])

        def ring(j):
            return j % (B - 2) if j % (B - 2) < 2 else 2 + (j - 2) % AHEAD

        block = ctx.enter_context(nc.Block())

        @block.sync
        def _(sp):
            def load_chunks(i):
                for c in range(C):
                    if i:
                        sp.wait_ge(xlo_done, C * (i - 1) + c + 1)
                        sp.wait_ge(xsum_done, i)
                    sp.dma_start(slot(x_stage, c), x_by4[i, :, c * H:(c + 1) * H]).then_inc(loaded_xc[c], 16)
                    if i:
                        sp.wait_ge(alo_done, C * (i - 1) + c + 1)
                    sp.dma_start(slot(a_stage, c), adj_by4[i, :, c * N:(c + 1) * N]).then_inc(loaded_ac[c], 16)

            def load_xa(i):
                sp.wait_ge(xlo_done, C * i)
                sp.wait_ge(xsum_done, i)
                sp.dma_start(slot(x_stage), x_by4[bass.ds(i, 1)].rearrange("b p f -> (b p) f")).then_inc(loaded_x, 16)
                sp.wait_ge(alo_done, C * i)
                sp.dma_start(slot(a_stage), adj_by4[bass.ds(i, 1)].rearrange("b p f -> (b p) f")).then_inc(loaded_a, 16)

            load_chunks(0)
            sp.dma_start(rw[:, :, :].rearrange("p e h -> p (e h)"), router_wt.partition_broadcast(P)).then_inc(loaded_const, 16)
            sp.dma_start(rb[:, :], router_b.partition_broadcast(P)).then_inc(loaded_const, 16)
            sp.dma_start(gb[:, 0], gamma).then_inc(loaded_const, 16)
            sp.dma_start(gb[:, 1], beta).then_inc(loaded_const, 16)
            load_chunks(1)
            sp.wait_ge(loaded_w, 16)
            sp.wait_ge(alo1_done, C - 1)
            with sp.Fori(2, B) as i:
                load_xa(i)

            def load_rows(j, q):
                sp.dma_start(slot(X0 + j).rearrange("p (c h) -> p c h", c=C),
                             x_rows[bass.ds(j, 1)].rearrange("b p c h -> (b p) c h")).then_inc(loaded_row[q], 16)

            def store_rows(j):
                sp.wait_ge(fin_done, FIN_DVE * (j + 1))
                sp.wait_ge(fin_a, FIN_ACT * (j + 1))
                sp.dma_start(out_rows[bass.ds(j, 1)].rearrange("b p c h -> (b p) c h"),
                             slot(X0 + j).rearrange("p (c h) -> p c h", c=C)).then_inc(stored, 16)

            sp.wait_ge(t_full, C * B)
            sp.wait_ge(loaded_w_last, 16)
            load_rows(0, 0)
            load_rows(1, 1)
            sp.wait_ge(o_full, C * (B - 1))
            load_rows(4, 4)
            load_rows(5, 5)
            sp.wait_ge(o_full, C * B)
            load_rows(2, 2)
            load_rows(3, 3)

            for j in range(2):
                sp.wait_ge(aff_v, through(AFF_DVE, 0, j))
                sp.wait_ge(aff_a, through(AFF_ACT, 0, j))
                load_rows(j + AHEAD, j + AHEAD)
            for j in range(2, B - AHEAD):
                store_rows(j - 2)
                sp.wait_ge(summed, C * (j + 1))
                load_rows(j + AHEAD, ring(j + AHEAD))
            for j in range(B - AHEAD - 2, B - BY_CHUNK):
                store_rows(j)
            for j in range(B - BY_CHUNK, B):
                for c in range(C):
                    if c < FIN_DVE or j == B - 1:
                        sp.wait_ge(fin_done, FIN_DVE * j + c + 1)
                    else:
                        sp.wait_ge(fin_a, FIN_ACT * j + c - FIN_DVE + 1)
                    sp.dma_start(out_rows[j, :, c, :], slot(X0 + j, c)).then_inc(stored, 16)
            sp.wait_ge(stored, 16 * (B - BY_CHUNK + BY_CHUNK * C))

        @block.gpsimd
        def _(pool):
            nc.gpsimd.memset(ident[:, :], 0.0).then_inc(ident_set, 1)
            pool.wait_ge(ident_set, 1)
            nc.gpsimd.affine_select(out=ident[:, :], in_=ident[:, :], compare_op=ALU.not_equal, fill=1.0, base=0,
                                    pattern=[[-1, P]], channel_multiplier=1).then_inc(ident_set, 1)
            nc.gpsimd.memset(minus_share[:, :], -1.0 / H).then_inc(share_set, 1)

            def load_w(i, first=False, last=False):
                pool.wait_ge(top1_done, i + 1)
                if last:
                    pool.wait_ge(t_full, C * B)
                elif not first:
                    pool.wait_ge(o_full, C * i)
                e = pool.value_load(top1[0:1, bass.ds(i, 1)], min_val=0, max_val=E - 1)
                pool.dma_start(slot(w_stage_last if last else w_stage).rearrange("p (c k) -> p c k", c=C),
                               w_v[bass.ds(e, 1)].rearrange("e p c k -> (e p) c k")).then_inc(loaded_w_last if last else loaded_w, 16)

            def sum_x(i, chunks=False):
                if chunks:
                    pool.wait_ge(loaded_xc[0], 16 * (i + 1))
                    pool.wait_ge(loaded_xc[1], 16 * (i + 1))
                else:
                    pool.wait_ge(loaded_x, 16 * (i - 1))
                if not (chunks and i == 0):
                    pool.wait_ge(racc_done, E * i)
                nc.gpsimd.tensor_tensor(xsum[:, :], slot(x_stage, 0), slot(x_stage, 1), ALU.add).then_inc(xsum_step, 1)
                for c in range(2, C):
                    if chunks:
                        pool.wait_ge(loaded_xc[c], 16 * (i + 1))
                    pool.wait_ge(xsum_step, (C - 2) * i + c - 1)
                    nc.gpsimd.tensor_tensor(xsum[:, :], xsum[:, :], slot(x_stage, c),
                                            ALU.add).then_inc(xsum_done if c == C - 1 else xsum_step, 1)

            sum_x(0, chunks=True)
            for c in range(C - 1):
                pool.wait_ge(ahi_done, C + c + 1)
                nc.gpsimd.tensor_tensor(alo[:, c, :], slot(a_stage, c), ahi[:, c, :].bitcast(F32),
                                        ALU.subtract).then_inc(alo1_done, 1)
            load_w(0, first=True)
            sum_x(1, chunks=True)
            with pool.Fori(1, B - 1) as i:
                sum_x(i + 1)
                load_w(i)
            load_w(B - 1, last=True)

            share = prod[:, 0:E * 2 * C * (B - FIRST)].rearrange("p (e s b) -> p e s b", e=E, s=2 * C)
            spread = abb[:, :, :, FIRST:].rearrange("p s c b -> p (s c) b")
            pool.wait_ge(coef_done, 1)
            nc.gpsimd.tensor_tensor(
                share, ab[:, :, :, :].rearrange("p e s c -> p e (s c)").unsqueeze(3).broadcast_to([P, E, 2 * C, B - FIRST]),
                mask[:, :, FIRST:].unsqueeze(2).broadcast_to([P, E, 2 * C, B - FIRST]), ALU.mult).then_inc(spread_step, 1)
            for e in range(1, E):
                pool.wait_ge(spread_step, e)
                nc.gpsimd.tensor_tensor(spread, spread if e > 1 else share[:, 0], share[:, e],
                                        ALU.add).then_inc(coef_done if e == E - 1 else spread_step, 1)

            def negative_means(j, q):
                pool.wait_ge(summed, C * (j + 1))
                if not (isinstance(j, int) and j < 2):
                    pool.wait_ge(fin_done, FIN_DVE * (j - 1))
                    pool.wait_ge(nmr_done, j - 1)
                nc.gpsimd.tensor_tensor(nm[q][:, :], s1[q][:, :], minus_share[:, :], ALU.mult).then_inc(nm_done, 1)

            def over_deviations(j, q):
                pool.wait_ge(nm_done, j + 1)
                pool.wait_ge(rs_done, j + 1)
                if not (isinstance(j, int) and j < 2):
                    pool.wait_ge(fin_a, FIN_ACT * (j - 1))
                nc.gpsimd.tensor_tensor(nmr[q][:, :], nm[q][:, :], rs[q][:, :], ALU.mult).then_inc(nmr_done, 1)

            pool.wait_ge(share_set, 1)
            negative_means(0, 0)
            negative_means(1, 1)
            over_deviations(0, 0)
            with pool.Fori(1, B // 2) as pair:
                for q in range(2):
                    negative_means(pair * 2 + q, q)
                    over_deviations(pair * 2 + q - 1, 1 - q)

        @block.scalar
        def _(act):
            def x_hi(i):
                act.wait_ge(loaded_x, 16 * (i - 1))
                act.wait_ge(t_full, C * i)
                for c in range(C):
                    nc.scalar.activation(xhi[:, c, :], slot(x_stage, c), ACT.Copy).then_inc(xhi_done, 1)

            def a_hi(i):
                act.wait_ge(loaded_a, 16 * (i - 1))
                act.wait_ge(t_full, C * i)
                for c in range(C):
                    nc.scalar.activation(ahi[:, c, :], slot(a_stage, c), ACT.Copy).then_inc(ahi_done, 1)

            def chunk_hi(i, c, x_part, a_part):
                act.wait_ge(loaded_xc[c], 16 * (i + 1))
                nc.scalar.activation(x_part[:, c, :], slot(x_stage, c), ACT.Copy).then_inc(xhi_done, 1)
                act.wait_ge(loaded_ac[c], 16 * (i + 1))
                nc.scalar.activation(a_part[:, c, :], slot(a_stage, c), ACT.Copy).then_inc(ahi_done, 1)

            def w_hi(i, first=False, last=False):
                if last:
                    act.wait_ge(loaded_w_last, 16)
                else:
                    act.wait_ge(loaded_w, 16 * (i + 1))
                if not first and not last:
                    act.wait_ge(o_full, C * i)
                for c in range(C):
                    nc.scalar.activation((whi_last if last else whi)[:, c, :], slot(w_stage_last if last else w_stage, c),
                                         ACT.Copy).then_inc(whi_done, 1)

            def t_hi(i, c, first=False):
                act.wait_ge(t_full, C * i + c + 1)
                if not first and c < C - 1:
                    act.wait_ge(t_used, (C - 1) * (i - 1) + c + 1)
                elif not first:
                    act.wait_ge(o_full, C * i)
                nc.scalar.activation(thi[:, c, :], t_bank[c][:, :], ACT.Copy).then_inc(thi_done, 1)

            def keep(i, last=False):
                for c in range(C):
                    if last:
                        act.wait_ge(bn_done, C * i + c + 1)
                    else:
                        act.wait_ge(o_full, C * i + c + 1)
                    nc.scalar.activation(slot(OUT0 + i, c), (t_bank if last else o_bank)[c][:, :], ACT.Copy).then_inc(o_kept, 1)

            def step(i, keeps=True, first=False):
                if keeps:
                    keep(i - 2)
                w_hi(i - 1, first)
                x_hi(i + 1)
                t_hi(i, 0)
                a_hi(i + 1)
                for c in range(1, C):
                    t_hi(i, c)

            act.wait_ge(const_set, 2)
            nc.scalar.activation(high[:, :], eps[:, :], ACT.Sqrt)
            for c in range(C):
                chunk_hi(0, c, xhi0, ahi0)
            for c in range(C):
                if c == C // 2:
                    t_hi(0, 0, first=True)
                chunk_hi(1, c, xhi, ahi)
            t_hi(0, 1, first=True)
            t_hi(0, 2, first=True)
            t_hi(0, 3, first=True)
            step(1, keeps=False, first=True)
            with act.Fori(2, B - 1) as i:
                step(i)
            keep(B - 3)
            w_hi(B - 2)
            t_hi(B - 1, 0)
            t_hi(B - 1, 1)
            w_hi(B - 1, last=True)
            t_hi(B - 1, 2)
            t_hi(B - 1, 3)
            keep(B - 2)
            keep(B - 1, last=True)

            act.wait_ge(var_done, 1)
            nc.scalar.activation(std[:, :, :], var[:, :, :], ACT.Sqrt, bias=eps[:, 0:1]).then_inc(std_done, 1)

            def affine(j, q, first=False):
                if not first:
                    act.wait_ge(turned, C * (j - 1))
                for c in range(AFF_DVE[q], C):
                    nc.scalar.activation(slot(T0 + q, c), slot(OUT0 + j, c), ACT.Identity,
                                         bias=abb[:, 1, c, bass.ds(j, 1)],
                                         scale=abb[:, 0, c, bass.ds(j, 1)]).then_inc(aff_a, 1)

            def final(j, q):
                act.wait_ge(nmr_done, j + 1)
                for c in range(FIN_DVE, C):
                    y = by_chunk[:, bass.ds((X0 + j) * C + c, 1), :].rearrange("p a n -> p (a n)")
                    nc.scalar.activation(y, y, ACT.Identity, bias=nmr[q][:, c:c + 1],
                                         scale=rs[q][:, c:c + 1]).then_inc(fin_a, 1)

            def rows(j, q):
                for c in range(C):
                    act.wait_ge(summed, C * j + c + 1)
                    nc.scalar.activation(squares[c], slot(X0 + j, c), ACT.Square, bias=s1[q][:, c:c + 1], scale=-float(H),
                                         accum_out=ssq[q][:, c:c + 1]).then_inc(sq_done, 1)
                act.wait_ge(sq_done, C * (j + 1))
                if not (isinstance(j, int) and j < 2):
                    act.wait_ge(rs_done, j - 1)
                nc.scalar.activation(sd[q][:, :], ssq[q][:, :], ACT.Sqrt, bias=eps[:, 0:1],
                                     scale=1.0 / H ** 3).then_inc(sd_done, 1)

            def rows_last():
                act.wait_ge(rs_done, B - 2)
                for c in range(C):
                    if c == 2:
                        final(B - 2, 0)
                    act.wait_ge(summed, C * (B - 1) + c + 1)
                    nc.scalar.activation(squares[c], slot(X0 + B - 1, c), ACT.Square, bias=s1[1][:, c:c + 1],
                                         scale=-float(H), accum_out=ssq[1][:, c:c + 1]).then_inc(sq_done, 1)
                    act.wait_ge(sq_done, C * (B - 1) + c + 1)
                    nc.scalar.activation(sd[1][:, c:c + 1], ssq[1][:, c:c + 1], ACT.Sqrt, bias=eps[:, 0:1],
                                         scale=1.0 / H ** 3).then_inc(sd_done, 1)

            act.wait_ge(coef_done, 1)
            affine(0, 0, first=True)
            affine(1, 1, first=True)
            rows(0, 0)
            act.wait_ge(coef_done, 2)
            affine(2, 0)
            rows(1, 1)
            final(0, 0)
            with act.Fori(2, B - 3, 2) as j0:
                for q in range(2):
                    affine(j0 + q + 1, 1 - q)
                    rows(j0 + q, q)
                    final(j0 + q - 1, 1 - q)
            affine(B - 1, 1)
            rows(B - 2, 0)
            final(B - 3, 1)
            rows_last()

        @block.vector
        def _(dve):
            nc.vector.memset(ones[:, :], 1.0).then_inc(const_set, 1)
            nc.vector.memset(eps[:, :], BN_EPS).then_inc(const_set, 1)
            for e in range(E):
                nc.vector.memset(iota[:, e:e + 1], float(e)).then_inc(const_set, 1)
                nc.vector.memset(down[:, e:e + 1], float(E - e)).then_inc(const_set, 1)

            def lo(dst, src, hi, c):
                return nc.vector.tensor_tensor(dst[:, c, :], slot(src, c), hi[:, c, :].bitcast(F32), ALU.subtract)

            def x_lo(i):
                for c in range(C):
                    dve.wait_ge(xhi_done, C * i + c + 1)
                    lo(xlo, x_stage, xhi, c).then_inc(xlo_done, 1)

            def a_lo(i):
                for c in range(C):
                    dve.wait_ge(ahi_done, C * i + c + 1)
                    lo(alo, a_stage, ahi, c).then_inc(alo_done, 1)

            def chunk_lo(i, c, x_parts, a_parts):
                dve.wait_ge(xhi_done, C * i + c + 1)
                lo(x_parts[1], x_stage, x_parts[0], c).then_inc(xlo_done, 1)
                if i and c < C - 1:
                    return
                dve.wait_ge(ahi_done, C * i + c + 1)
                lo(a_parts[1], a_stage, a_parts[0], c).then_inc(alo_done, C if i else 1)

            def w_lo(i, chunks=range(C), last=False):
                for c in chunks:
                    dve.wait_ge(whi_done, C * i + c + 1)
                    if last:
                        lo(wlo_last, w_stage_last, whi_last, c).then_inc(wlo_done, 1)
                    else:
                        lo(wlo, w_stage, whi, c).then_inc(wlo_done, 1)

            def t_lo(i, c):
                dve.wait_ge(thi_done, C * i + c + 1)
                nc.vector.tensor_tensor(tlo[:, c, :], t_bank[c][:, :], thi[:, c, :].bitcast(F32),
                                        ALU.subtract).then_inc(tlo_done, 1)

            def route(i, first=False):
                if first:
                    dve.wait_ge(loaded_const, 64)
                else:
                    dve.wait_ge(scores_done, i)
                dve.wait_ge(xsum_done, i + 1)
                for e in range(E):
                    if e or not first:
                        dve.wait_ge(racc_done, E * i + e)
                    nc.vector.tensor_tensor_reduce(junk[:, :], xsum[:, :], rw[:, e, :], 1.0, 0.0, ALU.mult, ALU.add,
                                                   racc[:, e:e + 1]).then_inc(racc_done, 1)

            def pick(i, first=False, bank=scores_ps):
                dve.wait_ge(scores_done, i + 1)
                if first:
                    dve.wait_ge(const_set, 2 + 2 * E)
                else:
                    dve.wait_ge(top1_done, i)
                nc.vector.scalar_tensor_tensor(scores[:, :], bank[:, 0:E], 1.0 / N, rb[:, :], ALU.mult,
                                               ALU.add).then_inc(scores_read, 1)
                dve.wait_ge(scores_read, i + 1)
                nc.vector.tensor_reduce(best[:, :], scores[:, :], AX_X, ALU.max).then_inc(best_done, 1)
                dve.wait_ge(best_done, i + 1)
                nc.vector.scalar_tensor_tensor(rank[:, :], scores[:, :], best[:, 0:1], down[:, :], ALU.is_ge,
                                               ALU.mult).then_inc(rank_done, 1)
                dve.wait_ge(rank_done, i + 1)
                nc.vector.tensor_reduce(high[:, :], rank[:, :], AX_X, ALU.max).then_inc(high_done, 1)
                dve.wait_ge(high_done, i + 1)
                nc.vector.tensor_scalar(top1[:, bass.ds(i, 1)], high[:, :], -1.0, float(E), ALU.mult,
                                        ALU.add).then_inc(top1_done, 1)

            def bn(i, first=False, last=False):
                for c in range(C):
                    if last:
                        dve.wait_ge(o_full, C * i + c + 1)
                    else:
                        dve.wait_ge(o_kept, C * i + c + 1)
                    if not first and not c:
                        dve.wait_ge(mv_done, 2 * i)
                    nc.vector.bn_stats(st6[:, c, :], t_bank[c][:, :] if last else slot(OUT0 + i, c)).then_inc(bn_done, 1)
                m, v = (st6[:, :, :].rearrange("p c (h s) -> p c h s", h=2)[:, :, :, t] for t in (1, 2))
                dve.wait_ge(bn_done, C * (i + 1))
                nc.vector.tensor_tensor(half_sq[:, :, :], m, m, ALU.mult).then_inc(half_step, 1)
                nc.vector.tensor_tensor(mv[:, bass.ds(i, 1), 0].rearrange("p b c -> p (b c)"), m[:, :, 0], m[:, :, 1],
                                        ALU.add).then_inc(mv_done, 1)
                dve.wait_ge(half_step, 2 * i + 1)
                nc.vector.scalar_tensor_tensor(half_sum[:, :, :], half_sq[:, :, :], N / 2, v, ALU.mult,
                                               ALU.add).then_inc(half_step, 1)
                dve.wait_ge(half_step, 2 * i + 2)
                nc.vector.tensor_tensor(mv[:, bass.ds(i, 1), 1].rearrange("p b c -> p (b c)"), half_sum[:, :, 0],
                                        half_sum[:, :, 1], ALU.add).then_inc(mv_done, 1)

            def step(i, stats=True, picks=True, w_chunks=range(C)):
                if stats:
                    bn(i - 2, first=isinstance(i, int) and i == 2)
                if picks:
                    pick(i)
                w_lo(i - 1, w_chunks)
                x_lo(i + 1)
                t_lo(i, 0)
                a_lo(i + 1)
                t_lo(i, 1)
                t_lo(i, 2)
                route(i + 1)
                t_lo(i, 3)

            for c in range(C):
                chunk_lo(0, c, (xhi0, xlo0), (ahi0, alo0))
            route(0, first=True)
            for c in range(C):
                if c == C // 2:
                    t_lo(0, 0)
                    pick(0, first=True, bank=o_bank[0])
                chunk_lo(1, c, (xhi, xlo), (ahi, alo))
            t_lo(0, 1)
            t_lo(0, 2)
            t_lo(0, 3)
            route(1)
            w_lo(0, range(1))
            pick(1, bank=o_bank[1])
            step(1, stats=False, picks=False, w_chunks=range(1, C))
            step(2)
            with dve.Fori(3, B - 1) as i:
                step(i)
            bn(B - 3)
            pick(B - 1)
            w_lo(B - 2)
            t_lo(B - 1, 0)
            t_lo(B - 1, 1)
            w_lo(B - 1, last=True)
            t_lo(B - 1, 2)
            t_lo(B - 1, 3)
            bn(B - 2)

            count = [0]

            def link(ins):
                count[0] += 1
                ins.then_inc(coef_step, 1)
                dve.wait_ge(coef_step, count[0])

            def affine(j, q, first=False):
                if not first:
                    dve.wait_ge(turned, C * (j - 1))
                for c in range(AFF_DVE[q]):
                    nc.vector.tensor_scalar(slot(T0 + q, c), slot(OUT0 + j, c), abb[:, 0, c, bass.ds(j, 1)],
                                            abb[:, 1, c, bass.ds(j, 1)], ALU.mult, ALU.add).then_inc(aff_v, 1)

            dve.wait_ge(top1_done, B)
            dve.wait_ge(mv_done, 2 * (B - 1))
            link(nc.vector.tensor_copy(top1f[:, :], top1[:, :]))
            link(nc.vector.tensor_tensor(mask[:, :, :], iota[:, :].unsqueeze(2).broadcast_to([P, E, B]),
                                         top1f[:, :].unsqueeze(1).broadcast_to([P, E, B]), ALU.is_equal))
            link(nc.vector.tensor_reduce(cnt[:, :], mask[:, :, :], AX_X, ALU.add))
            link(nc.vector.tensor_scalar(cnt[:, :], cnt[:, :], 1.0, None, ALU.max))
            link(nc.vector.reciprocal(rcnt[:, :], cnt[:, :]))
            for s, scale in enumerate((0.5, 1.0 / N)):
                link(nc.vector.scalar_tensor_tensor(weight[:, s], mask[:, :, :], scale,
                                                    rcnt[:, :].unsqueeze(2).broadcast_to([P, E, B]), ALU.mult, ALU.mult))
            for s in range(2):
                by_expert = prod[:, 0:E * C * (B - 1)].rearrange("p (e c b) -> p e c b", e=E, c=C)
                link(nc.vector.tensor_tensor(
                    by_expert, mv[:, 0:B - 1, s].rearrange("p b c -> p c b").unsqueeze(1).broadcast_to([P, E, C, B - 1]),
                    weight[:, s, :, 0:B - 1].unsqueeze(2).broadcast_to([P, E, C, B - 1]), ALU.mult))
                link(nc.vector.tensor_reduce(tot[:, :, s], by_expert, AX_X, ALU.add))
            bn(B - 1, last=True)
            dve.wait_ge(mv_done, 2 * B)
            link(nc.vector.tensor_tensor(last_share, mv[:, B - 1].unsqueeze(1).broadcast_to([P, E, 2, C]),
                                         weight[:, :, :, B - 1].rearrange("p s e -> p e s").unsqueeze(3).broadcast_to([P, E, 2, C]),
                                         ALU.mult))
            link(nc.vector.tensor_tensor(avg[:, :, :, :], tot[:, :, :, :], last_share, ALU.add))
            mean_e, sq_e = avg[:, :, 0], avg[:, :, 1]
            link(nc.vector.tensor_tensor(var[:, :, :], mean_e, mean_e, ALU.mult))
            nc.vector.tensor_tensor(var[:, :, :], sq_e, var[:, :, :], ALU.subtract).then_inc(var_done, 1)
            dve.wait_ge(std_done, 1)
            link(nc.vector.reciprocal(std[:, :, :], std[:, :, :]))
            link(nc.vector.tensor_tensor(ab[:, :, 0], std[:, :, :], gb[:, 0], ALU.mult))
            link(nc.vector.tensor_tensor(ab[:, :, 1], mean_e, ab[:, :, 0], ALU.mult))
            link(nc.vector.tensor_tensor(ab[:, :, 1], gb[:, 1], ab[:, :, 1], ALU.subtract))
            by_batch = prod[:, 0:2 * C * FIRST * E].rearrange("p (s b e) -> p s b e", s=2 * C, b=FIRST)
            link(nc.vector.tensor_tensor(
                by_batch, ab[:, :, :, :].rearrange("p e s c -> p (s c) e").unsqueeze(2).broadcast_to([P, 2 * C, FIRST, E]),
                mask[:, :, 0:FIRST].rearrange("p e b -> p b e").unsqueeze(1).broadcast_to([P, 2 * C, FIRST, E]), ALU.mult))
            nc.vector.tensor_reduce(abb[:, :, :, 0:FIRST].rearrange("p s c b -> p (s c) b"), by_batch, AX_X,
                                    ALU.add).then_inc(coef_done, 1)
            dve.wait_ge(coef_done, 1)
            affine(0, 0, first=True)
            affine(1, 1, first=True)

            def rows(j, q, l, rounds, before=True):
                dve.wait_ge(loaded_row[l], rounds * 16 + 16)
                for c in range(C):
                    if before and c == RECIP_AT:
                        deviations(j - 1, 1 - q)
                    dve.wait_ge(turned, C * j + c + 1)
                    nc.vector.scalar_tensor_tensor(slot(X0 + j, c), bank[C * q + c][:, :], 0.0, slot(X0 + j, c), ALU.max,
                                                   ALU.add, accum_out=s1[q][:, c:c + 1]).then_inc(summed, 1)

            def deviations(j, q):
                dve.wait_ge(sd_done, j + 1)
                if not (isinstance(j, int) and j < 2):
                    dve.wait_ge(fin_a, FIN_ACT * (j - 1))
                nc.vector.reciprocal(rs[q][:, :], sd[q][:, :]).then_inc(rs_done, 1)

            def final(j, q):
                dve.wait_ge(nm_done, j + 1)
                dve.wait_ge(rs_done, j + 1)
                for c in range(FIN_DVE):
                    nc.vector.tensor_scalar(slot(X0 + j, c), slot(X0 + j, c), nm[q][:, c:c + 1], rs[q][:, c:c + 1],
                                            ALU.add, ALU.mult).then_inc(fin_done, 1)

            rows(0, 0, 0, 0, before=False)
            dve.wait_ge(coef_done, 2)
            affine(2, 0)
            rows(1, 1, 1, 0)
            final(0, 0)
            with dve.Fori(0, (B - 4) // AHEAD) as r:
                for u in range(AHEAD):
                    j, q = r * AHEAD + 2 + u, u % 2
                    affine(j + 1, 1 - q)
                    rows(j, q, 2 + u, r)
                    final(j - 1, 1 - q)
            affine(B - 1, 1)
            rows(B - 2, 0, 0, 1)
            final(B - 3, 1)
            rows(B - 1, 1, 1, 1)
            final(B - 2, 0)
            dve.wait_ge(nm_done, B)
            dve.wait_ge(fin_a, FIN_ACT * (B - 2))
            for c in range(C):
                dve.wait_ge(sd_done, B - 1 + c + 1)
                nc.vector.reciprocal(rs[1][:, c:c + 1], sd[1][:, c:c + 1]).then_inc(rs_done, 1)
                dve.wait_ge(rs_done, B - 1 + c + 1)
                nc.vector.tensor_scalar(slot(X0 + B - 1, c), slot(X0 + B - 1, c), nm[1][:, c:c + 1], rs[1][:, c:c + 1],
                                        ALU.add, ALU.mult).then_inc(fin_done, 1)

        @block.tensor
        def _(pe):
            def product(dst, parts, start, stop):
                (shi, slo), (mhi, mlo) = parts
                nc.tensor.matmul(dst, shi, mhi, start=start, stop=False)
                nc.tensor.matmul(dst, shi, mlo, start=False, stop=False)
                return nc.tensor.matmul(dst, slo, mhi, start=False, stop=stop)

            def score(i, dst):
                pe.wait_ge(racc_done, E * (i + 1))
                nc.tensor.matmul(dst[:, 0:E], ones[:, :], racc[:, :], start=True, stop=True).then_inc(scores_done, 1)

            def aggregate_0():
                for m in range(C):
                    pe.wait_ge(alo_done, m + 1)
                    for h in range(C):
                        if m == C - 1 and h == C // 2:
                            score(0, o_bank[0])
                        cols = slice(h * P, (h + 1) * P)
                        mm = product(t_bank[h][:, :], ((xhi0[:, m, cols], xlo0[:, m, cols]), (ahi0[:, m, :], alo0[:, m, :])),
                                     m == 0, m == C - 1)
                        if m == C - 1:
                            mm.then_inc(t_full, 1)

            def aggregate_1():
                for h in range(C):
                    pe.wait_ge(tlo_done, h + 1)
                    for m in range(C):
                        if h == C - 1 and m == C // 2:
                            score(1, o_bank[1])
                        if h == 0 and m < C - 1:
                            pe.wait_ge(xlo_done, C + m + 1)
                            pe.wait_ge(alo1_done, m + 1)
                        elif h == 0:
                            pe.wait_ge(alo_done, C + 1)
                        cols = slice(h * P, (h + 1) * P)
                        mm = product(t_bank[h][:, :], ((xhi[:, m, cols], xlo[:, m, cols]), (ahi[:, m, :], alo[:, m, :])),
                                     m == 0, m == C - 1)
                    mm.then_inc(t_full, 1)

            def aggregate(i):
                pe.wait_ge(alo_done, C * (i + 1))
                for h in range(C):
                    pe.wait_ge(tlo_done, C * (i - 1) + h + 1)
                    if h == 1:
                        pe.wait_ge(tlo_done, C * i)
                        score(i, scores_ps)
                    if h == C - 1:
                        pe.wait_ge(scores_read, i + 1)
                    for m in range(C):
                        cols = slice(h * P, (h + 1) * P)
                        mm = product(t_bank[h][:, :], ((xhi[:, m, cols], xlo[:, m, cols]), (ahi[:, m, :], alo[:, m, :])),
                                     m == 0, m == C - 1)
                    mm.then_inc(t_full, 1)

            def project(i, first=False):
                if first:
                    pe.wait_ge(scores_read, 2)
                else:
                    pe.wait_ge(o_kept, C * i)
                for h in range(C):
                    pe.wait_ge(wlo_done, C * i + h + 1)
                    pe.wait_ge(tlo_done, C * i + h + 1)
                    for k in range(C):
                        cols = slice(k * P, (k + 1) * P)
                        mm = product(o_bank[k][:, :], ((whi[:, h, cols], wlo[:, h, cols]), (thi[:, h, :], tlo[:, h, :])),
                                     h == 0, h == C - 1)
                        if h == C - 1:
                            mm.then_inc(o_full, 1)
                    if h < C - 1:
                        mm.then_inc(t_used, 1)

            def warm_up(rounds):
                for _ in range(rounds):
                    nc.tensor.matmul(o_bank[C - 1][:, 0:P], ones[:, :], ones[:, :], start=True, stop=True)

            pe.wait_ge(const_set, 1)
            warm_up(11)
            aggregate_0()
            aggregate_1()
            project(0, first=True)
            with pe.Fori(2, B) as i:
                aggregate(i)
                project(i - 1)
            pe.wait_ge(wlo_done, C * B)
            for k in range(C):
                pe.wait_ge(tlo_done, C * (B - 1) + k + 1)
                for h in range(C):
                    if k == 0:
                        pe.wait_ge(tlo_done, C * (B - 1) + h + 1)
                    cols = slice(k * P, (k + 1) * P)
                    mm = product(t_bank[k][:, :], ((whi_last[:, h, cols], wlo_last[:, h, cols]), (thi[:, h, :], tlo[:, h, :])),
                                 h == 0, h == C - 1)
                mm.then_inc(o_full, 1)

            def turn(pair, q, first=False):
                j = pair * 2 + q
                pe.wait_ge(aff_v, through(AFF_DVE, pair, q))
                pe.wait_ge(aff_a, through(AFF_ACT, pair, q))
                for n in range(C):
                    if not first:
                        pe.wait_ge(summed, C * (j - 2) + n + 1)
                    for k in range(C):
                        mm = nc.tensor.transpose(bank[C * q + n][:, k * P:(k + 1) * P],
                                                 arena[:, (T0 + q) * SLOT + k * N + n * P:][:, 0:P], ident[:, :])
                    mm.then_inc(turned, 1)

            pe.wait_ge(o_kept, C * (B - 1))
            warm_up(22)
            pe.wait_ge(ident_set, 2)
            pe.wait_ge(o_kept, C * B)
            turn(0, 0, first=True)
            turn(0, 1, first=True)
            with pe.Fori(1, B // 2) as pair:
                for q in range(2):
                    turn(pair, q)


def kernel(x, adj, L0_gnn_router_w, L0_gnn_router_b, L0_gnn_expert_w, L0_gnn_bn_gamma, L0_gnn_bn_beta):
    import numpy as np
    import concourse.bacc as bacc
    from concourse import mybir as mb
    from concourse.bass_utils import run_bass_kernel_spmd

    E, H = L0_gnn_bn_gamma.shape
    layout = {
        "x": np.ascontiguousarray(x),
        "adj_t": np.ascontiguousarray(np.swapaxes(adj, 1, 2)),
        "w": np.ascontiguousarray(L0_gnn_expert_w),
        "router_wt": np.ascontiguousarray(np.transpose(L0_gnn_router_w)).reshape(-1),
        "router_b": np.ascontiguousarray(L0_gnn_router_b),
        "gamma": np.ascontiguousarray(np.transpose(np.reshape(L0_gnn_bn_gamma, (E, H // 128, 128)), (2, 0, 1))),
        "beta": np.ascontiguousarray(np.transpose(np.reshape(L0_gnn_bn_beta, (E, H // 128, 128)), (2, 0, 1))),
    }
    nc = bacc.Bacc("TRN2", target_bir_lowering=False, num_devices=1)
    aps = [nc.dram_tensor(f"{k}_dram", v.shape, mb.dt.float32, kind="ExternalInput").ap() for k, v in layout.items()]
    out = nc.dram_tensor("out_dram", layout["x"].shape, mb.dt.float32, kind="ExternalOutput").ap()
    build(nc, *aps, out)
    r = run_bass_kernel_spmd(nc, [{f"{k}_dram": v for k, v in layout.items()}], core_ids=[0])
    return r.results[0]["out_dram"]
```
